# Optimizing a Trainium2 kernel written in Bass

```python
import numpy as np
import jax
import jax.numpy as jnp

def _softmax(x, axis=-1):
    return jax.nn.softmax(x, axis=axis)

def _gelu(x):
    return jax.nn.gelu(x, approximate=True)

def _silu(x):
    return jax.nn.silu(x)

def _sigmoid(x):
    return jax.nn.sigmoid(x)

def _layernorm(x, axis=-1, eps=1e-05):
    m = jnp.mean(x, axis=axis, keepdims=True)
    v = jnp.var(x, axis=axis, keepdims=True)
    return (x - m) / jnp.sqrt(v + eps)

def _scatter_add(tgt, idx, src, axis=0):
    return tgt.at[idx].add(src)

def _segment_sum(src, seg, n):
    return jax.ops.segment_sum(src, seg, n)
kernel_name = 'mk_early_fusion_embed_d1_tok_img1024_r4_f1084b'

def setup_inputs(seed: int=0):
    np.random.seed(seed)
    _w = jnp.asarray

    def _rec_inputs():
        import jax
        import jax.numpy as jnp
        _rk = jax.random.key(seed)
        x = jax.random.uniform(jax.random.fold_in(_rk, 1), (8, 3, 256, 256), jnp.float32, 0.0, 1)
        x_txt = jax.random.randint(jax.random.fold_in(_rk, 51), (8, 128), 0, 31999, jnp.int32)
        return (x, x_txt)
    x, x_txt = _rec_inputs()

    def _L0_tok_setup():
        import jax, jax.numpy as jnp
        import numpy as np
        _GRAY_W = (0.2989, 0.587, 0.114)
        key = jax.random.key(seed)
        x = jax.random.uniform(key, (32, 3, 256, 256), dtype=jnp.float32)
        sx = jnp.array([[-3.0, 0.0, 3.0], [-10.0, 0.0, 10.0], [-3.0, 0.0, 3.0]], dtype=jnp.float32)
        scharr = jnp.stack([sx, sx.T])[:, None, :, :]
        return {'x': x, 'scharr': scharr}
    _L0_tok_all = _L0_tok_setup()
    _L0_tok_in = {k: v for k, v in _L0_tok_all.items() if k in ('scharr',)}
    del _L0_tok_all

    def _L0_txt_setup():
        import jax, jax.numpy as jnp
        import numpy as np
        VOCAB = 8000
        EMBED = 256
        RANK = 16
        ALPHA = 16
        SCALING = ALPHA / RANK
        key = jax.random.key(seed)
        k_x, k_w, k_a = jax.random.split(key, 3)
        x = jax.random.randint(k_x, (4, 1024), 0, VOCAB, dtype=jnp.int32)
        base_weight = jax.random.normal(k_w, (EMBED, VOCAB), dtype=jnp.float32) * 0.02
        lora_A = jax.random.normal(k_a, (VOCAB, RANK), dtype=jnp.float32) * 0.02
        lora_B = jnp.zeros((RANK, EMBED), dtype=jnp.float32)
        return {'x': x, 'base_weight': base_weight, 'lora_A': lora_A, 'lora_B': lora_B}
    _L0_txt_all = _L0_txt_setup()
    _L0_txt_in = {k: v for k, v in _L0_txt_all.items() if k in ('base_weight', 'lora_A', 'lora_B')}
    del _L0_txt_all

    def _L0_attn_setup():
        import jax, jax.numpy as jnp
        import numpy as np
        DIM_EMB = 256
        NUM_HEADS = 16
        DIM_HEAD = DIM_EMB // NUM_HEADS
        key = jax.random.key(seed)
        k1, k2, k3 = jax.random.split(key, 3)
        x = jax.random.normal(k1, (4, 512, DIM_EMB), dtype=jnp.float32)
        w_qkv = jax.random.normal(k2, (3 * NUM_HEADS * DIM_HEAD, DIM_EMB), dtype=jnp.float32) * DIM_EMB ** (-0.5)
        w_out = jax.random.normal(k3, (DIM_EMB, NUM_HEADS * DIM_HEAD), dtype=jnp.float32) * (NUM_HEADS * DIM_HEAD) ** (-0.5)
        return {'x': x, 'w_qkv': w_qkv, 'w_out': w_out}
    _L0_attn_all = _L0_attn_setup()
    _L0_attn_in = {k: v for k, v in _L0_attn_all.items() if k in ('w_qkv', 'w_out')}
    del _L0_attn_all

    def _L0_ffn_setup():
        import jax, jax.numpy as jnp
        import numpy as np
        B, S, D, E, F, K = (4, 256, 256, 8, 704, 1)
        key = jax.random.key(seed)
        ks = jax.random.split(key, 8)
        sc = 0.02
        return {'x_bsD': jax.random.normal(ks[0], (B, S, D), jnp.float32), 'router_DE': jax.random.normal(ks[1], (D, E), jnp.float32) * sc, 'w1_eDF': jax.random.normal(ks[2], (E, D, F), jnp.float32) * sc, 'w3_eDF': jax.random.normal(ks[3], (E, D, F), jnp.float32) * sc, 'w2_eFD': jax.random.normal(ks[4], (E, F, D), jnp.float32) * sc, 'ws1_DF': jax.random.normal(ks[5], (D, F), jnp.float32) * sc, 'ws3_DF': jax.random.normal(ks[6], (D, F), jnp.float32) * sc, 'ws2_FD': jax.random.normal(ks[7], (F, D), jnp.float32) * sc}
    _L0_ffn_all = _L0_ffn_setup()
    _L0_ffn_in = {k: v for k, v in _L0_ffn_all.items() if k in ('router_DE', 'w1_eDF', 'w3_eDF', 'w2_eFD', 'ws1_DF', 'ws3_DF', 'ws2_FD')}
    del _L0_ffn_all
    return {'x': x, 'x_txt': x_txt, 'L0_tok_scharr': _L0_tok_in['scharr'], 'L0_txt_base_weight': _L0_txt_in['base_weight'], 'L0_txt_lora_A': _L0_txt_in['lora_A'], 'L0_txt_lora_B': _L0_txt_in['lora_B'], 'L0_attn_w_qkv': _L0_attn_in['w_qkv'], 'L0_attn_w_out': _L0_attn_in['w_out'], 'L0_ffn_router_DE': _L0_ffn_in['router_DE'], 'L0_ffn_w1_eDF': _L0_ffn_in['w1_eDF'], 'L0_ffn_w3_eDF': _L0_ffn_in['w3_eDF'], 'L0_ffn_w2_eFD': _L0_ffn_in['w2_eFD'], 'L0_ffn_ws1_DF': _L0_ffn_in['ws1_DF'], 'L0_ffn_ws3_DF': _L0_ffn_in['ws3_DF'], 'L0_ffn_ws2_FD': _L0_ffn_in['ws2_FD']}

def reference(x, x_txt, L0_tok_scharr, L0_txt_base_weight, L0_txt_lora_A, L0_txt_lora_B, L0_attn_w_qkv, L0_attn_w_out, L0_ffn_router_DE, L0_ffn_w1_eDF, L0_ffn_w3_eDF, L0_ffn_w2_eFD, L0_ffn_ws1_DF, L0_ffn_ws3_DF, L0_ffn_ws2_FD):
    import jax
    import jax.numpy as jnp

    def _L0_tok_ref(x, scharr):
        import jax, jax.numpy as jnp
        import numpy as np
        _GRAY_W = (0.2989, 0.587, 0.114)
        w = jnp.asarray(_GRAY_W, dtype=x.dtype)
        gray = jnp.einsum('bchw,c->bhw', x, w)[:, None]
        edges = jax.lax.conv_general_dilated(gray, scharr, window_strides=(1, 1), padding='SAME', dimension_numbers=('NCHW', 'OIHW', 'NCHW'))
        abs_edges = jnp.sqrt(jnp.square(edges))
        edge = abs_edges.sum(axis=1) / 2
        return edge

    def _L0_txt_ref(x, base_weight, lora_A, lora_B):
        import jax, jax.numpy as jnp
        import numpy as np
        VOCAB = 8000
        EMBED = 256
        RANK = 16
        ALPHA = 16
        SCALING = ALPHA / RANK
        x_emb = base_weight.T[x]
        lora = jnp.einsum('bsr,re->bse', lora_A[x], lora_B)
        return x_emb + lora * SCALING

    def _L0_attn_ref(x, w_qkv, w_out):
        import jax, jax.numpy as jnp
        import numpy as np
        DIM_EMB = 256
        NUM_HEADS = 16
        DIM_HEAD = DIM_EMB // NUM_HEADS
        b, t, _ = x.shape
        scale = DIM_HEAD ** (-0.5)
        qkv = jnp.einsum('bte,fe->btf', x, w_qkv)
        qkv = qkv.reshape(b, t, 3, NUM_HEADS, DIM_HEAD)
        q, k, v = (qkv[:, :, 0], qkv[:, :, 1], qkv[:, :, 2])
        scores = jnp.einsum('bihd,bjhd->bhij', q, k) * scale
        weights = jax.nn.softmax(scores, axis=-1)
        attn = jnp.einsum('bhij,bjhd->bhid', weights, v)
        concat = attn.transpose(0, 2, 1, 3).reshape(b, t, NUM_HEADS * DIM_HEAD)
        return jnp.einsum('btf,ef->bte', concat, w_out)

    def _L0_ffn_ref(x_bsD, router_DE, w1_eDF, w3_eDF, w2_eFD, ws1_DF, ws3_DF, ws2_FD):
        import jax, jax.numpy as jnp
        import numpy as np
        B, S, D, E, F, K = (4, 256, 256, 8, 704, 1)
        b, s, d = x_bsD.shape
        a = b * s
        x_aD = x_bsD.reshape(a, d)
        scores_aE = x_aD @ router_DE
        vals_aK, idx_aK = jax.lax.top_k(scores_aE, K)
        masked_aE = jnp.full_like(scores_aE, -jnp.inf).at[jnp.arange(a)[:, None], idx_aK].set(vals_aK)
        gates_Ea = jax.nn.sigmoid(masked_aE).T
        routed_in_EaD = jax.lax.stop_gradient(gates_Ea[:, :, None] * x_aD[None, :, :])
        mid_EaF = jax.nn.silu(jnp.einsum('ead,edf->eaf', routed_in_EaD, w1_eDF)) * jnp.einsum('ead,edf->eaf', routed_in_EaD, w3_eDF)
        routed_out_EaD = jnp.einsum('eaf,efd->ead', mid_EaF, w2_eFD)
        shared_aD = jax.nn.silu(x_aD @ ws1_DF) * (x_aD @ ws3_DF) @ ws2_FD
        out_aD = shared_aD + routed_out_EaD.sum(axis=0)
        return out_aD.reshape(b, s, d)
    h = _L0_tok_ref(x, L0_tok_scharr)
    h = jnp.concatenate([h, _L0_txt_ref(x_txt, L0_txt_base_weight, L0_txt_lora_A, L0_txt_lora_B)], axis=1)
    h = h + _L0_attn_ref(_layernorm(h, axis=-1), L0_attn_w_qkv, L0_attn_w_out)
    h = h + _L0_ffn_ref(_layernorm(h, axis=-1), L0_ffn_router_DE, L0_ffn_w1_eDF, L0_ffn_w3_eDF, L0_ffn_w2_eFD, L0_ffn_ws1_DF, L0_ffn_ws3_DF, L0_ffn_ws2_FD)
    return h

_drawn_inputs = setup_inputs


def setup_inputs(seed=0):
    import zlib

    import numpy as np

    out = dict(_drawn_inputs(seed))
    spreads = {'L0_txt_lora_B': (0.0, 0.1)}
    factors = {'L0_ffn_router_DE': 8.0,
     'L0_ffn_w1_eDF': 8.0,
     'L0_ffn_w3_eDF': 8.0,
     'L0_ffn_w2_eFD': 8.0,
     'L0_ffn_ws1_DF': 4.722,
     'L0_ffn_ws3_DF': 4.672,
     'L0_ffn_ws2_FD': 4.692}
    for name, (base, spread) in spreads.items():
        noise = np.random.default_rng([zlib.crc32(name.encode()), seed]).standard_normal(out[name].shape)
        drawn = base * np.exp(spread * noise) if base else spread * noise
        out[name] = jnp.asarray(drawn.astype(out[name].dtype))
    for name, factor in factors.items():
        out[name] = (out[name] * factor).astype(out[name].dtype)
    return out
```

```python
from contextlib import ExitStack

import concourse.bass as bass
from concourse import mybir

ALU = mybir.AluOpType
ACT = mybir.ActivationFunctionType
AX = mybir.AxisListType
F32 = mybir.dt.float32
F32R = mybir.dt.float32r
BF16 = mybir.dt.bfloat16
I32 = mybir.dt.int32

P = 128
EPS = 1e-5
GRAY = (0.2989, 0.587, 0.114)

USES = [
    (0, "attn_back", 3, -1), (0, "shift", 1, 0),
    (1, "xT", 0, 1), (1, "xT", 1, 1),
    (2, "attnT", 0, -1), (2, "attnT", 1, -1),
    (3, "qk", 0, 1), (4, "qk", 2, 1), (4, "proj", 0, -1), (5, "qk", 1, 1), (5, "proj", 1, -1),
    (6, "qk", 3, 1), (6, "shift", 2, 0), (6, "proj", 2, -1),
    (8, "attn_back", 0, 0),
    (9, "x2T", 0, -1), (9, "x2T", 1, -1),
    (10, "router", 0, -1),
    (11, "gate", 0, -1), (11, "up", 0, -1),
    (12, "shift", 3, 0), (12, "gate", 1, -1), (12, "up", 1, -1),
    (13, "gate", 2, -1), (13, "up", 2, -1),
    (14, "attn_back", 1, 0), (14, "gate", 3, -1), (14, "up", 3, -1),
    (15, "gate", 4, -1), (15, "up", 4, -1),
    (16, "gate", 5, -1), (16, "up", 5, -1),
    (18, "shift", 0, 1),
    (19, "down", 0, -1),
    (20, "attn_back", 2, 0),
    (21, "down", 1, -1),
    (23, "down", 2, -1),
    (24, "v", 0, 1), (24, "v", 1, 1), (24, "v", 2, 1),
]
BANK = {(what, n): i % 3 for i, (_, what, n, _) in enumerate(USES)}
PROLOGUE = [("loraT", 0), ("loraT", 1), ("lora", 0), ("lora", 1), ("lora", 2), ("lora", 3),
            ("xT", 0), ("xT", 1), ("qk", 0), ("qk", 2), ("qk", 1), ("qk", 3), ("shift", 0),
            ("v", 0), ("v", 1), ("v", 2)]
for _i, _u in enumerate(PROLOGUE[:6]):
    BANK[_u] = _i % 3
PLACE = {("qk", 0): 0, ("qk", 2): 1, ("qk", 1): 2, ("qk", 3): 3}
HALVES = 24


class Signal:

    def __init__(self, sem, per, by=1):
        self.sem, self.per, self.by = sem, per, by

    def at(self, batch, n=None):
        return (batch * self.per + (self.per if n is None else n + 1)) * self.by


def embed_block_moe_kernel(nc, x, x_txt, scharr, base_rows, lora_A, lora_B, w_qkvT, w_outT, router,
                           w1, w3, w2, ws1, ws3, ws2, out):
    NB, C, IMG, D = x.shape
    TXT = x_txt.shape[1]
    TOK = IMG + TXT
    NT = TOK // P
    HEADS = 16
    DH = D // HEADS
    VOCAB, RANK = lora_A.shape
    E, _, F = w1.shape
    NF = (F + P - 1) // P
    FT = [min(P, F - P * f) for f in range(NF)]
    DC = D // P
    G = 4
    NG = HEADS // G
    NTOK = NB * TOK
    COLS = NB * NT
    TILES = NTOK // P + E - 1
    HF = F // 2
    PARTS = [(0, 0), (0, 1), (0, 2), (1, 0), (1, 1), (2, 0)]
    KROWS = len(PARTS) * DH
    assert TILES % 2 == 1 and NT == 3 and DC == 2 and DH == 16 and KROWS + 3 <= P and HF <= 512 and HF % 2 == 0

    parts_dram = nc.dram_tensor("parts_dram", [3, 4, P, TOK], BF16).ap()
    shift_dram = nc.dram_tensor("shift_dram", [3, HEADS, TOK], BF16).ap()
    gated_dram = nc.dram_tensor("gated_dram", [NB, TOK, D], F32).ap()

    ctx = ExitStack()
    with ctx:
        def sb(name, shape, dt, scope=ctx):
            return scope.enter_context(nc.sbuf_tensor(name, shape, dt))

        def ps(name, shape, dt):
            return ctx.enter_context(nc.psum_tensor(name, shape, dt))

        def signal(name, per, by=1):
            return Signal(ctx.enter_context(nc.semaphore(name)), per, by)

        def sem(name):
            return ctx.enter_context(nc.semaphore(name))

        st_ps = ps("st_ps", [P, 2, 512], F32)
        sm_ps = ps("sm_ps", [P, 2, 512], F32)
        pv_ps = ps("pv_ps", [P, 512], F32)
        work = ps("work", [P, 3, 512], F32)

        ident = sb("ident", [P, P], F32)
        identb = sb("identb", [P, P], BF16)
        before = sb("before", [P, P], BF16)
        onesb = sb("onesb", [P, P], BF16)
        iota_p = sb("iota_p", [P, P], F32)
        iota_t = sb("iota_t", [P, TILES], F32)
        iota_e = sb("iota_e", [P, E], F32)
        iota_k = sb("iota_k", [P, COLS], F32)
        lower_e = sb("lower_e", [P, E, E], F32)
        token = sb("token", [P, NB, NT], I32)
        scores8 = sb("scores8", [P, COLS, E], F32)
        slot_of = sb("slot_of", [P, TILES], I32)
        route_i = sb("route_i", [1, 2 * TILES + E], I32)
        arena = sb("arena", [P, 14592], F32)
        at = [0]

        def room(words):
            at[0] += words
            return arena[:, at[0] - words:at[0]]

        q_st = room(HEADS * TOK // 2).bitcast(BF16).rearrange("p (h t) -> p h t", h=HEADS)
        k_st = room(HEADS * TOK // 2).bitcast(BF16).rearrange("p (h t) -> p h t", h=HEADS)
        parts = room(6 * TOK).bitcast(BF16).rearrange("p (a m t) -> p a m t", a=3, m=4)
        v_sb = room(NT * HEADS * 2 * DH).rearrange("p (t h d) -> p t h d", t=NT, h=HEADS)
        probs_room = room(3 * G * TOK)
        probs = probs_room.rearrange("p (s g t) -> p s g t", s=3, g=G)
        at[0] = 0
        wx = [room(3 * n * w).rearrange("p (s c w) -> p s c w", s=3, c=n) for n, w in ((DC, F), (DC, F), (NF, D))]
        raw = [probs_room[:, i * NF * D:(i + 1) * NF * D] for i in range(2)]
        text_room = probs_room[:, 2 * NF * D:3 * NF * D]
        lora_a = text_room[:, 0:NB * RANK].rearrange("p (b r) -> p b r", b=NB)
        lora_b = text_room[0:RANK, NB * RANK:NB * RANK + D]
        lora_aT = text_room[0:RANK, NB * RANK + D:NB * RANK + D + NB * P]
        x_in = sb("x_in", [P, C, 2, D], F32)
        product = sb("product", [P, 2, 2, D], F32)
        gray = sb("gray", [P, 4, D + 2], F32)
        edge = sb("edge", [P, 2, 2, D], F32)
        taps = sb("taps", [P, 2, 9], F32)
        h = sb("h", [P, COLS, D], F32)
        xn = sb("xn", [P, NT, D], F32)
        xn2 = sb("xn2", [P, NT, D], F32)
        xT = [sb(f"xT_{s}", [P, DC, TOK], F32R) for s in ("high", "low")]
        attnT = [sb(f"attnT_{s}", [P, DC, TOK], F32R) for s in ("high", "low")]
        x2T = attnT
        mid = [sb(f"mid_{s}", [P, NF, TOK], F32R) for s in ("high", "low")]
        mid_f = sb("mid_f", [P, 2, TOK], F32)
        tanh = sb("tanh", [P, 2, TOK], F32)
        half_u = sb("half_u", [P, TOK], F32)
        rest = sb("rest", [P, TOK], F32)
        attn = sb("attn", [P, NT, D], F32)
        ot = sb("ot", [P, TOK], F32)
        stats = sb("stats", [P, 2, NT, 6], F32)
        mv = sb("mv", [P, 2, NT, 2], F32)
        rstd = sb("rstd", [P, 2, NT], F32)
        smax = sb("smax", [P, NT, G], F32)
        smax_r = sb("smax_r", [P, NT, G], F32)
        shift_p = sb("shift_p", [P, NT, 3, G], BF16)
        shift_T = sb("shift_T", [3 * G, TOK], BF16)
        rden = sb("rden", [P, NT, G], F32)
        best = sb("best", [P, NT], F32)
        gate = sb("gate", [P, NT], F32)
        wqkv = [sb(f"wqkv_{s}", [P, DC, 3 * D], F32R) for s in ("high", "low")]
        wo = [sb(f"wo_{s}", [P, DC, D], F32R) for s in ("high", "low")]
        wr = [sb(f"wr_{s}", [P, DC, E], F32R) for s in ("high", "low")]
        wg = [sb(f"wg_{s}", [P, DC, F], F32R) for s in ("high", "low")]
        wu = [sb(f"wu_{s}", [P, DC, F], F32R) for s in ("high", "low")]
        wd = [sb(f"wd_{s}", [P, NF, D], F32R) for s in ("high", "low")]
        ids = sb("ids", [P, NB], I32)
        ids_n = sb("ids_n", [P, NB], I32)

        consts_made = sem("consts_made")
        sp_passed, pool_passed, dve_passed = sem("sp_passed"), sem("pool_passed"), sem("dve_passed")
        small_in = sem("small_in")
        weights_in = [sem(f"weights_in{i}") for i in range(6)]
        ids_step = sem("ids_step")
        text_in = sem("text_in")
        lora_in = sem("lora_in")
        w_high = sem("w_high")
        w_split = sem("w_split")
        x_loaded = signal("x_loaded", 1, 16)
        picture0_step = sem("picture0_step")
        gray_begun = signal("gray_begun", 1)
        product_made = signal("product_made", 18)
        product_added = signal("product_added", 18)
        halo_in = signal("halo_in", 2, 16)
        first_tap = signal("first_tap", 2)
        edge_step = signal("edge_step", 3)
        ln_stats = [signal(f"ln{i}_stats", 3) for i in (1, 2)]
        ln_aggr = [signal(f"ln{i}_aggr", 3) for i in (1, 2)]
        ln_rstd = [signal(f"ln{i}_rstd", 2) for i in (1, 2)]
        ln_done = [signal(f"ln{i}_done", 3) for i in (1, 2)]
        KINDS = {"attn_back": 4, "shift": 4, "xT": 2, "attnT": 2, "qk": 4, "proj": 3, "x2T": 2,
                 "router": 1, "gate": 6, "up": 6, "down": 3, "v": 3, "loraT": 2, "lora": 4}
        made = {k: signal(f"{k}_made", n) for k, n in KINDS.items()}
        taken = {k: signal(f"{k}_taken", n) for k, n in KINDS.items()}
        high = {k: signal(f"{k}_high", KINDS[k]) for k in ("xT", "attnT", "x2T", "qk")}
        tanh_made = signal("tanh_made", 6)
        mid_high = signal("mid_high", 6)
        mid_low = signal("mid_low", 6)
        part2_made = signal("part2_made", 4)
        parts_made = signal("parts_made", 4)
        parts_out = signal("parts_out", 4, 16)
        stack_in = [signal(f"stack_in{g}", 12, 16) for g in range(NG)]
        smax_made = signal("smax_made", 12 * NG)
        smax_found = signal("smax_found", 12 * NG)
        shift_step = signal("shift_step", 3 * NG)
        shift_split = signal("shift_split", NG)
        shift_out = signal("shift_out", NG, 16)
        shift_in = [signal(f"shift_in{g}", 3, 16) for g in range(NG)]
        st_made = signal("st_made", 12 * NG)
        exp_made = signal("exp_made", 12 * NG)
        pv_made = signal("pv_made", 12)
        ot_copied = signal("ot_copied", 4)
        rden_made = signal("rden_made", 4)
        best_found = signal("best_found", 1)
        gate_exp = signal("gate_exp", 1)
        gate_step = signal("gate_step", 2)
        gated_made = signal("gated_made", 3)
        gated_out = signal("gated_out", 2, 16)
        rows_out = signal("rows_out", 2, 16)
        route_step = sem("route_step")
        routed = sem("routed")
        rank_made = sem("rank_made")
        slots_made = sem("slots_made")
        expert_in = [sem(f"expert_in{i}") for i in range(2)]
        expert_ready = sem("expert_ready")
        row_in = [sem(f"row_in{i}") for i in range(2)]
        row_cleared = sem("row_cleared")
        e_xT = sem("e_xT")
        e_xT_copied = sem("e_xT_copied")
        e_gate_made = sem("e_gate_made")
        e_up = sem("e_up")
        e_tanh = sem("e_tanh")
        e_u = sem("e_u")
        e_mid = sem("e_mid")
        e_midT = sem("e_midT")
        e_midT_a = sem("e_midT_a")
        e_midT_b = sem("e_midT_b")
        e_down = sem("e_down")
        e_y = sem("e_y")
        row_out = [sem(f"row_out{i}") for i in range(2)]

        x_room = x_in[:, :, :, :].rearrange("p c r w -> p (c r w)")
        xg = x_room[:, 0:2 * D].rearrange("p (i d) -> p i d", i=2)
        y_e = x_room[:, 2 * D:4 * D].rearrange("p (i d) -> p i d", i=2)
        xT_e = x_room[:, 4 * D:5 * D]
        tanh_e = gray[:, :, :].rearrange("p r w -> p (r w)")[:, 0:F].rearrange("p (i n) -> p i n", i=2)
        u_e = edge[:, :, :, :].rearrange("p f r w -> p (f r w)")[:, 0:F].rearrange("p (i n) -> p i n", i=2)
        mid_row = xn[:, :, :].rearrange("p t d -> p (t d)")[:, 0:F]
        mid_e = mid_row.rearrange("p (i n) -> p i n", i=2)
        midT_e = xn2[:, :, :].rearrange("p t d -> p (t d)")
        t_room = tanh[:, :, :].rearrange("p i t -> p (i t)")
        rt_a = t_room[:, 0:COLS * E].rearrange("p (c e) -> p c e", c=COLS)
        rt_e24 = t_room[:, COLS * E:2 * COLS * E].rearrange("p (e c) -> p e c", e=E)
        rt_te = t_room[:, 2 * COLS * E:2 * COLS * E + TILES * E].rearrange("p (t e) -> p t e", t=TILES)
        rt_ee = t_room[:, 640:640 + E * E].rearrange("p (e c) -> p e c", e=E)
        rt_b = half_u[:, 0:P]
        rt_small = rest[:, 0:64]
        rt_i = rest[:, 64:128].bitcast(I32)
        onehot = rest[:, 128:128 + COLS * E // 2].bitcast(BF16).rearrange("p (c e) -> p c e", c=COLS)
        tile_hot = attn[:, :, :].rearrange("p t d -> p (t d)")[:, 0:COLS * TILES].rearrange("p (c t) -> p c t", c=COLS)
        tile_val = mid_f[:, :, :].rearrange("p i t -> p (i t)")[:, 0:COLS * TILES].bitcast(BF16)\
            .rearrange("p (c i t) -> p c i t", c=COLS, i=2)
        slot_hot = xn[:, :, :].rearrange("p t d -> p (t d)").bitcast(BF16).rearrange("p (c s) -> p c s", c=12)
        slot_i = sb("slot_i", [P, 4], I32)
        minus_half = sb("minus_half", [P, NT], F32)
        gated_rows = gated_dram.rearrange("b t d -> (b t) d")
        out_rows = out.rearrange("b t d -> (b t) d")
        ids_in = sem("ids_in")
        taps_halved = sem("taps_halved")
        onehot_made = sem("onehot_made")
        slot_cols = sem("slot_cols")
        slots_read = sem("slots_read")
        slot_picked = sem("slot_picked")
        CONSTS, CORE_CONSTS, SPLITS, PICTURE0 = 18, 10, 7, 21
        LOW_AT = {12 + f: f for f in range(NF)}

        def gray_rows(k):
            dy, dx = divmod(k, 3)
            return gray[:, dy:dy + 2, dx:dx + D]

        def uses_of(phase):
            if phase == "prologue":
                return [(None, what, n, 1) for what, n in PROLOGUE]
            front, back, core_ = phase != NB - 1 and phase != "end", phase != 0, phase != "end"
            return [u for u in USES if {1: front, 0: core_, -1: back}[u[3]]]

        def phase_before(phase):
            return {"prologue": None, 0: "prologue", "loop": "loop", NB - 2: "loop",
                    NB - 1: NB - 2, "end": NB - 1}[phase]

        def wait_bank(pe, phase, j, what, n):
            seq = uses_of(phase)
            at = [(u[1], u[2]) for u in seq].index((what, n))
            back = 0
            while True:
                at -= 1
                if at < 0:
                    phase, back = phase_before(phase), back + 1
                    if phase is None:
                        return
                    seq = uses_of(phase)
                    at = len(seq) - 1
                if BANK[seq[at][1], seq[at][2]] == BANK[what, n]:
                    break
            _, kind, m, ahead = seq[at]
            batch = 0 if kind in ("lora", "loraT") else j - back + ahead
            pe.wait_ge(taken[kind].sem, taken[kind].at(batch, PLACE.get((kind, m), m)))

        def bank(what, n):
            return work[:, BANK[what, n], :]

        def head_rows(g):
            return g // 2, (g % 2) * G * DH

        block = ctx.enter_context(nc.Block())

        @block.sync
        def _(sp):
            def load_x(b):
                if isinstance(b, int) and b == 1:
                    sp.wait_ge(picture0_step, 3)
                elif not isinstance(b, int) or b > 1:
                    sp.wait_ge(product_made.sem, product_made.at(b - 2, 1))
                sp.dma_start(x_in[:, :, :, :].rearrange("p c r w -> p c (r w)"),
                             x[bass.ds(b, 1)].rearrange("a c (p r) w -> p (a c) (r w)", r=2)
                             ).then_inc(x_loaded.sem, 16)

            def load_halo(b):
                if isinstance(b, int) and b == 0:
                    sp.wait_ge(picture0_step, 3)
                else:
                    sp.wait_ge(product_added.sem, product_added.at(b - 1, 1))
                sp.dma_start(gray[1:P, 0, 1:D + 1], gray[0:P - 1, 2, 1:D + 1]).then_inc(halo_in.sem, 16)
                sp.dma_start(gray[0:P - 1, 3, 1:D + 1], gray[1:P, 1, 1:D + 1]).then_inc(halo_in.sem, 16)

            def write_parts(b):
                if not (isinstance(b, int) and b == 0):
                    for g in range(NG):
                        sp.wait_ge(stack_in[g].sem, stack_in[g].at(b - 1))
                for m in (0, 2, 1, 3):
                    sp.wait_ge(parts_made.sem, parts_made.at(b, PLACE["qk", m]))
                    sp.dma_start(parts_dram[:, m].rearrange("a p t -> p a t"), parts[:, :, m, :]
                                 ).then_inc(parts_out.sem, 16)

            def load_stack(b, g):
                sp.wait_ge(parts_out.sem, parts_out.at(b))
                sp.sem_inc(sp_passed, 1)
                if not (isinstance(b, int) and b == 0):
                    sp.wait_ge(st_made.sem, st_made.at(b - 1, 12 * g + 11))
                m, row = head_rows(g)
                for i, (pq, pk) in enumerate(PARTS):
                    for dst, part, tile in ((q_st, pq, m), (k_st, pk, 2 + m)):
                        sp.dma_start(dst[DH * i:DH * i + DH, G * g:G * g + G, :],
                                     parts_dram[part, tile, row:row + G * DH, :]
                                     .rearrange("(h d) t -> d h t", d=DH)).then_inc(stack_in[g].sem, 16)

            def move_shift(b, g):
                sp.wait_ge(taken["shift"].sem, taken["shift"].at(b, g))
                sp.dma_start(shift_dram[:, G * g:G * g + G, :], shift_T[:, :]).then_inc(shift_out.sem, 16)
                sp.wait_ge(shift_out.sem, shift_out.at(b, g))
                for a in range(3):
                    sp.dma_start(q_st[KROWS + a:KROWS + a + 1, G * g:G * g + G, :],
                                 shift_dram[a:a + 1, G * g:G * g + G, :]).then_inc(shift_in[g].sem, 16)

            def store_rows(dram, picture, text, b, done):
                pic = dram[bass.ds(b, 1), 0:IMG, :].rearrange("a (p r) d -> p (a r) d", r=2)
                sp.dma_start(pic, picture).then_inc(done.sem, 16)
                txt = dram[bass.ds(b, 1), IMG:TOK, :].rearrange("a p d -> p (a d)")
                sp.dma_start(txt, text).then_inc(done.sem, 16)

            def store_gated(b):
                sp.wait_ge(gated_made.sem, gated_made.at(b))
                store_rows(gated_dram, xn2[:, 0:2, :], xn2[:, 2, :], b, gated_out)

            def store_out(b):
                sp.wait_ge(taken["down"].sem, taken["down"].at(b))
                store_rows(out, h[:, bass.ds(b * NT, 2), :], h[:, bass.ds(b * NT + 2, 1), :].rearrange("p a d -> p (a d)"),
                           b, rows_out)

            def load_weight(i, dst, src):
                sp.dma_start(dst, src).then_inc(weights_in[i], 16)

            load_x(0)
            with nc.allow_non_contiguous_dma(reason="1024 token numbers"):
                sp.dma_start(ids[:, :], x_txt.rearrange("b t -> t b")).then_inc(ids_in, 16)
            sp.dma_start(lora_b, lora_B).then_inc(small_in, 16)
            sp.dma_start(taps[:, :, :].rearrange("p f k -> p (f k)"),
                         scharr.rearrange("f a u v -> (f a u v)").partition_broadcast(P)
                         ).then_inc(small_in, 16)
            load_weight(0, raw[0][:, 0:DC * 3 * D].rearrange("p (c n) -> p c n", c=DC),
                        w_qkvT.rearrange("(c p) n -> p c n", p=P))
            load_weight(1, raw[1][:, 0:DC * D].rearrange("p (c n) -> p c n", c=DC),
                        w_outT.rearrange("(c p) n -> p c n", p=P))
            load_weight(1, raw[1][:, DC * D:DC * D + DC * E].rearrange("p (c n) -> p c n", c=DC),
                        router.rearrange("(c p) n -> p c n", p=P))
            load_halo(0)
            load_x(1)
            load_halo(1)
            sp.wait_ge(w_split, 1)
            load_weight(2, raw[0][:, 0:DC * F].rearrange("p (c n) -> p c n", c=DC),
                        ws1.rearrange("(c p) n -> p c n", p=P))
            sp.wait_ge(w_split, 3)
            load_weight(3, raw[1][:, 0:DC * F].rearrange("p (c n) -> p c n", c=DC),
                        ws3.rearrange("(c p) n -> p c n", p=P))
            sp.wait_ge(w_split, 4)
            load_weight(4, raw[0][:, 0:(NF - 1) * D].rearrange("p (c n) -> p c n", c=NF - 1),
                        ws2[0:(NF - 1) * P, :].rearrange("(c p) n -> p c n", p=P))
            load_weight(4, raw[0][0:FT[-1], (NF - 1) * D:NF * D], ws2[(NF - 1) * P:F, :])
            write_parts(0)
            for g in range(NG):
                load_stack(0, g)
            move_shift(0, 0)

            def body(j, front, back, conv, carry):
                f, b = j + 1, j - 1
                if conv:
                    load_x(j + 2)
                if carry:
                    load_stack(j, 3)
                move_shift(j, 1)
                if conv:
                    load_halo(j + 2)
                if front:
                    write_parts(f)
                if front:
                    load_stack(f, 0)
                move_shift(j, 2)
                if back:
                    store_gated(b)
                if front:
                    load_stack(f, 1)
                move_shift(j, 3)
                if front:
                    load_stack(f, 2)
                    move_shift(f, 0)
                if back:
                    store_out(b)

            body(0, True, False, True, False)
            with sp.Fori(1, NB - 2) as j:
                body(j, True, True, True, True)
            body(NB - 2, True, True, False, True)
            body(NB - 1, False, True, False, True)

            def load_expert(e):
                sl = e % 3
                sp.dma_start(wx[0][:, sl], w1[e].rearrange("(c p) n -> p c n", p=P)).then_inc(expert_in[e % 2], 16)
                sp.dma_start(wx[1][:, sl], w3[e].rearrange("(c p) n -> p c n", p=P)).then_inc(expert_in[e % 2], 16)
                sp.dma_start(wx[2][:, sl, 0:NF - 1], w2[e, 0:(NF - 1) * P, :].rearrange("(c p) n -> p c n", p=P)
                             ).then_inc(expert_in[e % 2], 16)
                sp.dma_start(wx[2][0:FT[-1], sl, NF - 1], w2[e, (NF - 1) * P:F, :]).then_inc(expert_in[e % 2], 16)

            sp.wait_ge(pv_made.sem, pv_made.at(NB - 1))
            for e in range(3):
                load_expert(e)
                if e:
                    sp.wait_ge(expert_in[(e - 1) % 2], 64 * ((e - 1) // 2 + 1))
                    sp.sem_inc(expert_ready, 1)
                if e == 0:
                    store_gated(NB - 1)
                    store_out(NB - 1)
            sp.wait_ge(routed, 1)
            for e in range(3, E):
                first = sp.value_load(route_i[0:1, 2 * TILES + e - 2:2 * TILES + e - 1], min_val=0, max_val=TILES)
                sp.wait_ge(e_down, first)
                load_expert(e)
                sp.wait_ge(expert_in[(e - 1) % 2], 64 * ((e - 1) // 2 + 1))
                sp.sem_inc(expert_ready, 1)
            sp.wait_ge(expert_in[(E - 1) % 2], 64 * ((E - 1) // 2 + 1))
            sp.sem_inc(expert_ready, 1)

        @block.gpsimd
        def _(pool):
            made_n = [0]

            def const(ins):
                made_n[0] += 1
                ins.then_inc(consts_made, 1)

            const(nc.gpsimd.memset(gray[:, :, :], 0.0))
            const(nc.gpsimd.memset(ident[:, :], 0.0))
            const(nc.gpsimd.memset(identb[:, :], 0.0))
            const(nc.gpsimd.memset(onesb[:, :], 1.0))
            pool.wait_ge(consts_made, made_n[0])
            const(nc.gpsimd.memset(k_st[KROWS:KROWS + 3], 1.0))
            pool.wait_ge(consts_made, made_n[0])
            const(nc.gpsimd.memset(v_sb, 1.0))
            const(nc.gpsimd.memset(minus_half[:, :], -0.5))
            pool.wait_ge(consts_made, made_n[0])
            const(nc.gpsimd.affine_select(out=ident[:, :], in_=ident[:, :], compare_op=ALU.not_equal, fill=1.0,
                                          base=0, pattern=[[-1, P]], channel_multiplier=1))
            const(nc.gpsimd.affine_select(out=identb[:, :], in_=identb[:, :], compare_op=ALU.not_equal, fill=1.0,
                                          base=0, pattern=[[-1, P]], channel_multiplier=1))
            const(nc.gpsimd.affine_select(out=before[:, :], in_=onesb[:, :], compare_op=ALU.is_gt, fill=0.0,
                                          base=0, pattern=[[1, P]], channel_multiplier=-1))

            def add_product(b, n):
                pool.wait_ge(product_made.sem, product_made.at(b - 1, n))
                if not (isinstance(b, int) and b == 1 and n == 0):
                    pool.wait_ge(product_added.sem, product_added.at(b - 1, n - 1))
                into = gray[:, 1:3, 1:D + 1] if n < 2 else edge[:, (n - 2) // 8]
                nc.gpsimd.tensor_tensor(into, into, product[:, n % 2], ALU.add).then_inc(product_added.sem, 1)

            def norm_scale(which, b):
                pool.wait_ge(ln_aggr[which].sem, ln_aggr[which].at(b))
                pool.sem_inc(pool_passed, 1)
                nc.gpsimd.tensor_scalar(rstd[:, which, :], mv[:, which, :, 1], EPS, None, ALU.add
                                        ).then_inc(ln_rstd[which].sem, 1)
                pool.wait_ge(ln_rstd[which].sem, ln_rstd[which].at(b, 0))
                nc.gpsimd.tensor_tensor(rstd[:, which, :], rstd[:, which, :], minus_half[:, :], ALU.pow
                                        ).then_inc(ln_rstd[which].sem, 1)

            def low_mid(b, f):
                n = FT[f]
                pool.wait_ge(mid_high.sem, mid_high.at(b, f))
                nc.gpsimd.tensor_tensor(mid[1][0:n, f, :], mid_f[0:n, f % 2, :], mid[0][0:n, f, :].bitcast(F32),
                                        ALU.subtract).then_inc(mid_low.sem, 1)

            pool.wait_ge(ids_step, 3)
            for b in range(NB):
                nc.gpsimd.indirect_dma_start(h[:, NT * b + 2, :], None, base_rows[:, :],
                                             bass.IndirectOffsetOnAxis(ids[:, b:b + 1], 0)).then_inc(text_in, 16)
                nc.gpsimd.indirect_dma_start(lora_a[:, b, :], None, lora_A[:, :],
                                             bass.IndirectOffsetOnAxis(ids[:, b:b + 1], 0)).then_inc(lora_in, 16)
            norm_scale(0, 0)
            for n in range(18):
                add_product(1, n)
            const(nc.gpsimd.iota(iota_p[:, :], [[1, P]], base=0, channel_multiplier=0, allow_small_or_imprecise_dtypes=True))
            const(nc.gpsimd.iota(iota_t[:, :], [[1, TILES]], base=0, channel_multiplier=0, allow_small_or_imprecise_dtypes=True))
            const(nc.gpsimd.iota(iota_e[:, :], [[1, E]], base=-E, channel_multiplier=0, allow_small_or_imprecise_dtypes=True))
            const(nc.gpsimd.iota(iota_k[:, :], [[P, COLS]], base=0, channel_multiplier=0, allow_small_or_imprecise_dtypes=True))
            const(nc.gpsimd.memset(lower_e[:, :, :], 1.0))
            pool.wait_ge(consts_made, made_n[0])
            const(nc.gpsimd.affine_select(out=lower_e[:, :, :], in_=lower_e[:, :, :], compare_op=ALU.is_gt, fill=0.0,
                                          base=0, pattern=[[1, E], [-1, E]], channel_multiplier=0))
            const(nc.gpsimd.iota(token[:, :, 0:2], [[TOK, NB], [1, 2]], base=-NTOK, channel_multiplier=2))
            const(nc.gpsimd.iota(token[:, :, 2:3], [[TOK, NB]], base=IMG - NTOK, channel_multiplier=1))
            assert made_n[0] == CONSTS
            norm_scale(0, 1)

            def body(j, back, conv):
                b, c = j - 1, j + 2
                for q in range(HALVES):
                    if q == 0 and conv:
                        add_product(c, 0)
                        add_product(c, 1)
                    if q == 8 and back:
                        norm_scale(1, b)
                    if q in LOW_AT and back:
                        low_mid(b, LOW_AT[q])
                    if 4 <= q < 20 and conv:
                        add_product(c, q - 2)
                    if q == 21 and conv:
                        norm_scale(0, c)

            body(0, False, True)
            with pool.Fori(1, NB - 2) as j:
                body(j, True, True)
            body(NB - 2, True, False)
            body(NB - 1, True, False)
            norm_scale(1, NB - 1)
            for f in range(NF):
                low_mid(NB - 1, f)

            def gather(k, i):
                nc.gpsimd.indirect_dma_start(xg[:, i, :], None, gated_rows,
                                             bass.IndirectOffsetOnAxis(slot_i[:, i:i + 1], 0),
                                             bounds_check=NTOK - 1, oob_is_err=False).then_inc(row_in[i], 16)

            def pick_slots(k, i, n):
                nc.gpsimd.tensor_copy(slot_i[:, i:i + 1], slot_of[:, bass.ds(k, 1)]).then_inc(slot_picked, 1)
                pool.wait_ge(slot_picked, n)
                pool.sem_inc(pool_passed, 1)

            def scatter(k, i, n):
                if not (isinstance(k, int) and k < 2):
                    pool.wait_ge(row_out[i], (k - i) * 8)
                pick_slots(k, 2 + i, n)
                pool.wait_ge(e_y, k + 1)
                pool.sem_inc(pool_passed, 1)
                nc.gpsimd.indirect_dma_start(out_rows, bass.IndirectOffsetOnAxis(slot_i[:, 2 + i:3 + i], 0), y_e[:, i, :],
                                             None, bounds_check=NTOK - 1, oob_is_err=False, compute_op=ALU.add
                                             ).then_inc(row_out[i], 16)

            nc.gpsimd.memset(xg, 0.0).then_inc(row_cleared, 1)
            pool.wait_ge(row_cleared, 1)
            pool.wait_ge(routed, 1)
            pool.wait_ge(gated_out.sem, gated_out.at(NB - 1))
            pool.wait_ge(rows_out.sem, rows_out.at(NB - 1))
            for i in range(2):
                pick_slots(i, i, i + 1)
                gather(i, i)

            def turn(k, i, last):
                if not last:
                    pool.wait_ge(e_xT, k + 2)
                    pick_slots(k + 3, 1 - i, 2 * k + 4)
                    gather(k + 3, 1 - i)
                    scatter(k, i, 2 * k + 5)
                else:
                    scatter(k, i, TILES + k + 1)

            pool.wait_ge(e_xT, 1)
            pick_slots(2, 0, 3)
            gather(2, 0)
            turn(0, 0, False)
            turn(1, 1, False)
            with pool.Fori(2, TILES - 4, 2) as k:
                turn(k, 0, False)
                turn(k + 1, 1, False)
            turn(TILES - 3, 0, True)
            turn(TILES - 2, 1, True)
            turn(TILES - 1, 0, True)
            pool.wait_ge(row_out[0], 16 * (TILES // 2 + 1))
            pool.wait_ge(row_out[1], 16 * (TILES // 2))

        @block.scalar
        def _(act):
            def begin_gray(b):
                act.wait_ge(x_loaded.sem, x_loaded.at(b))
                if isinstance(b, int) and b == 1:
                    act.wait_ge(picture0_step, PICTURE0)
                nc.scalar.activation(gray[:, 1:3, 1:D + 1], x_in[:, 0], ACT.Copy, scale=GRAY[0]
                                     ).then_inc(gray_begun.sem, 1)

            def make_product(b, n):
                if not (isinstance(b, int) and b == 1 and n < 2):
                    act.wait_ge(product_added.sem, product_added.at(b - 1, n - 2))
                if n < 2:
                    act.wait_ge(gray_begun.sem, gray_begun.at(b - 1))
                    nc.scalar.activation(product[:, n % 2], x_in[:, n + 1], ACT.Copy, scale=GRAY[n + 1]
                                         ).then_inc(product_made.sem, 1)
                else:
                    f, k = divmod(n - 2, 8)
                    nc.scalar.activation(product[:, n % 2], gray_rows(k + 1), ACT.Copy, scale=taps[:, f, k + 1:k + 2]
                                         ).then_inc(product_made.sem, 1)

            def first_taps(b):
                act.wait_ge(halo_in.sem, halo_in.at(b))
                act.wait_ge(edge_step.sem, edge_step.at(b - 1))
                for f in range(2):
                    nc.scalar.activation(edge[:, f], gray_rows(0), ACT.Copy, scale=taps[:, f, 0:1]
                                         ).then_inc(first_tap.sem, 1)
                act.wait_ge(first_tap.sem, first_tap.at(b - 1))

            def exps(j, step, half):
                for hh in (2 * half, 2 * half + 1):
                    act.wait_ge(st_made.sem, st_made.at(j, 4 * step + hh))
                    if not (isinstance(j, int) and j == 0 and step < 3):
                        act.wait_ge(pv_made.sem, pv_made.at(j, step - 3))
                    nc.scalar.activation(probs[:, step % 3, hh, :], st_ps[:, hh % 2, 0:TOK], ACT.Exp,
                                         scale=DH ** -0.5).then_inc(exp_made.sem, 1)

            def copy_high(kind, n, b, dst):
                act.wait_ge(made[kind].sem, made[kind].at(b, n))
                nc.scalar.activation(dst[0][:, n, :], bank(kind, n)[:, 0:TOK], ACT.Copy).then_inc(high[kind].sem, 1)

            def copy_ot(j, g):
                act.wait_ge(pv_made.sem, pv_made.at(j, 3 * g + 2))
                if not (isinstance(j, int) and j == 0 and g == 0):
                    act.wait_ge(made["attn_back"].sem, made["attn_back"].at(j, g - 1))
                nc.scalar.activation(ot[:, :], pv_ps[:, 0:TOK], ACT.Copy).then_inc(ot_copied.sem, 1)

            def copy_shift(b, g):
                act.wait_ge(made["shift"].sem, made["shift"].at(b, g))
                if not (isinstance(b, int) and b == 0 and g == 0):
                    act.wait_ge(shift_out.sem, shift_out.at(b, g - 1))
                nc.scalar.activation(shift_T[:, :], bank("shift", g).bitcast(BF16)[0:3 * G, 0:TOK], ACT.Copy
                                     ).then_inc(taken["shift"].sem, 1)

            def part1(b, m):
                n = PLACE["qk", m]
                act.wait_ge(made["qk"].sem, made["qk"].at(b, n))
                if not (isinstance(b, int) and b == 0):
                    act.wait_ge(parts_out.sem, parts_out.at(b - 1))
                nc.scalar.activation(parts[:, 0, m, :], bank("qk", m)[:, 0:TOK], ACT.Copy).then_inc(high["qk"].sem, 1)

            def copy_v(b, t):
                act.wait_ge(made["v"].sem, made["v"].at(b, t))
                if not (isinstance(b, int) and b == 0):
                    act.wait_ge(pv_made.sem, pv_made.at(b - 1))
                nc.scalar.activation(v_sb[:, t, :, 0:DH], bank("v", t)[:, 0:D].rearrange("p (h d) -> p h d", h=HEADS),
                                     ACT.Copy).then_inc(taken["v"].sem, 1)

            def tanh_of(b, f):
                act.wait_ge(made["gate"].sem, made["gate"].at(b, f))
                act.wait_ge(taken["gate"].sem, taken["gate"].at(b, f - 2) if f >= 2 else taken["gate"].at(b - 1))
                n = FT[f]
                nc.scalar.activation(tanh[0:n, f % 2, :], bank("gate", f)[0:n, 0:TOK], ACT.Tanh, scale=0.5
                                     ).then_inc(tanh_made.sem, 1)

            def high_mid(b, f):
                act.wait_ge(taken["up"].sem, taken["up"].at(b, f))
                if not (isinstance(b, int) and b == 0):
                    act.wait_ge(made["down"].sem, made["down"].at(b - 1))
                n = FT[f]
                nc.scalar.activation(mid[0][0:n, f, :], mid_f[0:n, f % 2, :], ACT.Copy).then_inc(mid_high.sem, 1)

            def gate_exponential(b):
                act.wait_ge(best_found.sem, best_found.at(b))
                if not (isinstance(b, int) and b == 0):
                    act.wait_ge(gated_made.sem, gated_made.at(b - 1))
                nc.scalar.activation(gate[:, :], best[:, :], ACT.Exp, scale=-1.0).then_inc(gate_exp.sem, 1)

            act.wait_ge(taps_halved, 1)
            for n in range(2):
                act.wait_ge(made["loraT"].sem, n + 1)
                nc.scalar.activation(lora_aT[:, 4 * P * n:4 * P * n + 4 * P], bank("loraT", n)[0:RANK, :], ACT.Copy
                                     ).then_inc(taken["loraT"].sem, 1)
            begin_gray(1)
            for n in range(2):
                make_product(1, n)
            for n in range(2):
                copy_high("xT", n, 0, xT)
            for m in (0, 2, 1, 3):
                part1(0, m)
            first_taps(1)
            for n in range(2, 18):
                make_product(1, n)
            copy_shift(0, 0)
            act.wait_ge(consts_made, CORE_CONSTS)
            for t in range(NT):
                copy_v(0, t)
            act.wait_ge(w_split, SPLITS)

            def body(j, front, back, conv, end=False):
                f, b, c = j + 1, j - 1, j + 2
                for q in range(HALVES):
                    if not end:
                        exps(j, q // 2, q % 2)
                    if q in (6, 12, 18) and not end:
                        copy_ot(j, q // 6 - 1)
                    if q == 0 and conv:
                        begin_gray(c)
                        make_product(c, 0)
                        make_product(c, 1)
                    if q == 4 and conv:
                        first_taps(c)
                    if 4 <= q < 20 and conv:
                        make_product(c, q - 2)
                    for at_q, what, n, ahead in USES:
                        if at_q != q or not {1: front, 0: not end, -1: back}[ahead]:
                            continue
                        if what == "shift":
                            copy_shift(j + ahead, n)
                        elif what == "xT":
                            copy_high("xT", n, f, xT)
                        elif what == "attnT":
                            if n == 0 and not (isinstance(b, int) and b == 0):
                                act.wait_ge(made["up"].sem, made["up"].at(b - 1))
                            copy_high("attnT", n, b, attnT)
                        elif what == "x2T":
                            if n == 0:
                                act.wait_ge(made["proj"].sem, made["proj"].at(b))
                            copy_high("x2T", n, b, x2T)
                        elif what == "qk":
                            part1(f, n)
                        elif what == "gate":
                            tanh_of(b, n)
                            if n == 0:
                                gate_exponential(b)
                            if n >= 1:
                                high_mid(b, n - 1)
                    if q == 17 and back:
                        high_mid(b, NF - 1)
                if not end:
                    copy_ot(j, 3)
                if front:
                    for t in range(NT):
                        copy_v(f, t)

            body(0, True, False, True)
            with act.Fori(1, NB - 2) as j:
                body(j, True, True, True)
            body(NB - 2, True, True, False)
            body(NB - 1, False, True, False)
            body(NB, False, True, False, end=True)

            def e_transposed(k):
                act.wait_ge(e_xT, k + 1)
                if not (isinstance(k, int) and k == 0):
                    act.wait_ge(e_up, k)
                nc.scalar.activation(xT_e, pv_ps[:, 0:D], ACT.Copy).then_inc(e_xT_copied, 1)

            def e_gate(k):
                act.wait_ge(e_gate_made, k + 1)
                if not (isinstance(k, int) and k == 0):
                    act.wait_ge(e_u, k)
                nc.scalar.activation(tanh_e, st_ps[:, :, 0:HF], ACT.Tanh, scale=0.5).then_inc(e_tanh, 1)

            def e_mid_transposed(k):
                act.wait_ge(e_midT, k + 1)
                if not (isinstance(k, int) and k == 0):
                    act.wait_ge(e_down, k)
                nc.scalar.activation(midT_e[:, 0:4 * P], work[:, 0, :], ACT.Copy).then_inc(e_midT_a, 1)

            def e_result(k, i):
                act.wait_ge(e_down, k + 1)
                if not (isinstance(k, int) and k < 2):
                    act.wait_ge(row_out[i], (k - i) * 8)
                nc.scalar.activation(y_e[:, i, :], work[:, 2, 0:D], ACT.Copy).then_inc(e_y, 1)

            e_transposed(0)
            e_gate(0)
            e_transposed(1)
            def two_tiles(k):
                for i in (1, 0):
                    kk = k + 1 - i
                    e_gate(kk)
                    e_mid_transposed(kk - 1)
                    e_transposed(kk + 1)
                    e_result(kk - 1, 1 - i)

            two_tiles(1)
            with act.Fori(3, TILES - 2, 2) as k:
                two_tiles(k)
            for kk in (TILES - 2, TILES - 1):
                e_gate(kk)
                e_mid_transposed(kk - 1)
                if kk < TILES - 1:
                    e_transposed(kk + 1)
                e_result(kk - 1, (kk - 1) % 2)
            e_mid_transposed(TILES - 1)
            e_result(TILES - 1, 0)

        @block.vector
        def _(dve):
            V = nc.vector
            dve.wait_ge(ids_in, 16)
            V.tensor_scalar(ids_n[:, :], ids[:, :], 0, VOCAB, ALU.is_lt, ALU.mult).then_inc(ids_step, 1)
            dve.wait_ge(ids_step, 1)
            V.tensor_tensor(ids_n[:, :], ids_n[:, :], ids[:, :], ALU.add).then_inc(ids_step, 1)
            dve.wait_ge(ids_step, 2)
            V.tensor_scalar(ids[:, :], ids_n[:, :], VOCAB - 1, 0, ALU.min, ALU.max).then_inc(ids_step, 1)

            splits = [0]

            def split(dst, src, loaded, count):
                dve.wait_ge(weights_in[loaded], count)
                splits[0] += 1
                V.tensor_copy(dst[0], src).then_inc(w_high, 1)
                dve.wait_ge(w_high, splits[0])
                V.tensor_tensor(dst[1], src, dst[0].bitcast(F32), ALU.subtract).then_inc(w_split, 1)

            def as3(room_, c):
                return room_.rearrange("p (c n) -> p c n", c=c)

            def edges(b):
                for f in range(2):
                    if isinstance(b, int) and b == 0:
                        dve.wait_ge(picture0_step, PICTURE0)
                    else:
                        dve.wait_ge(product_added.sem, product_added.at(b - 1, 9 + 8 * f))
                    V.scalar_tensor_tensor(out=edge[:, f], in0=edge[:, f], scalar=-1.0, in1=edge[:, f],
                                           op0=ALU.mult, op1=ALU.max).then_inc(edge_step.sem, 1)
                dve.wait_ge(edge_step.sem, edge_step.at(b, 1))
                V.tensor_tensor(h[:, bass.ds(b * NT, 2), :], edge[:, 0], edge[:, 1], ALU.add).then_inc(edge_step.sem, 1)

            def norm_stats(which, b):
                if not (isinstance(b, int) and b == 0):
                    dve.wait_ge(ln_done[which].sem, ln_done[which].at(b - 1))
                dve.sem_inc(dve_passed, 1)
                for t in range(NT):
                    V.bn_stats(stats[:, which, t, :], h[:, bass.ds(b * NT + t, 1), :].rearrange("p a d -> p (a d)")
                               ).then_inc(ln_stats[which].sem, 1)
                for t in range(NT):
                    dve.wait_ge(ln_stats[which].sem, ln_stats[which].at(b, t))
                    dve.sem_inc(dve_passed, 1)
                    V.bn_aggr(mv[:, which, t, :], stats[:, which, t, :]).then_inc(ln_aggr[which].sem, 1)

            def norm_apply(which, b, dst):
                dve.wait_ge(ln_rstd[which].sem, ln_rstd[which].at(b))
                for t in range(NT):
                    V.tensor_scalar(dst[:, t, :], h[:, bass.ds(b * NT + t, 1), :].rearrange("p a d -> p (a d)"),
                                    mv[:, which, t, 0:1], rstd[:, which, t:t + 1], ALU.subtract, ALU.mult
                                    ).then_inc(ln_done[which].sem, 1)

            def low_part(kind, n, b, dst):
                dve.wait_ge(high[kind].sem, high[kind].at(b, n))
                V.tensor_tensor(dst[1][:, n, :], bank(kind, n)[:, 0:TOK], dst[0][:, n, :].bitcast(F32), ALU.subtract
                                ).then_inc(taken[kind].sem, 1)

            def parts23(b, m):
                n = PLACE["qk", m]
                dve.wait_ge(high["qk"].sem, high["qk"].at(b, n))
                if not (isinstance(b, int) and b == 0 and n == 0):
                    dve.wait_ge(parts_made.sem, parts_made.at(b, n - 1))
                V.tensor_tensor(rest[:, :], bank("qk", m)[:, 0:TOK], parts[:, 0, m, :], ALU.subtract
                                ).then_inc(taken["qk"].sem, 1)
                dve.wait_ge(taken["qk"].sem, taken["qk"].at(b, n))
                V.tensor_copy(parts[:, 1, m, :], rest[:, :]).then_inc(part2_made.sem, 1)
                dve.wait_ge(part2_made.sem, part2_made.at(b, n))
                V.tensor_tensor(parts[:, 2, m, :], rest[:, :], parts[:, 1, m, :], ALU.subtract
                                ).then_inc(parts_made.sem, 1)

            def maxima(b, g, i):
                hh, t = divmod(i, NT)
                n = 12 * g + i
                if i == 0 and not (isinstance(b, int) and b == 0 and g == 0):
                    dve.wait_ge(shift_split.sem, shift_split.at(b, g - 1))
                dve.wait_ge(smax_made.sem, smax_made.at(b, n))
                V.reduce_max(smax[:, t, hh:hh + 1], sm_ps[:, n % 2, 0:TOK], axis=AX.X).then_inc(smax_found.sem, 1)

            def split_shift(b, g):
                dve.wait_ge(smax_found.sem, smax_found.at(b, 12 * g + 11))
                if not (isinstance(b, int) and b == 0 and g == 0):
                    dve.wait_ge(made["shift"].sem, made["shift"].at(b, g - 1))
                V.tensor_scalar(shift_p[:, :, 0, :], smax[:, :, :], -1.0, None, ALU.mult).then_inc(shift_step.sem, 1)
                dve.wait_ge(shift_step.sem, shift_step.at(b, 3 * g))
                V.scalar_tensor_tensor(out=smax_r[:, :, :], in0=smax[:, :, :], scalar=-1.0, in1=shift_p[:, :, 0, :],
                                       op0=ALU.mult, op1=ALU.subtract).then_inc(shift_step.sem, 1)
                dve.wait_ge(shift_step.sem, shift_step.at(b, 3 * g + 1))
                V.tensor_copy(shift_p[:, :, 1, :], smax_r[:, :, :]).then_inc(shift_step.sem, 1)
                dve.wait_ge(shift_step.sem, shift_step.at(b, 3 * g + 2))
                V.tensor_tensor(shift_p[:, :, 2, :], smax_r[:, :, :], shift_p[:, :, 1, :], ALU.subtract
                                ).then_inc(shift_split.sem, 1)

            def normalise(j, g):
                dve.wait_ge(made["attn_back"].sem, made["attn_back"].at(j, g))
                if not (isinstance(j, int) and j == 0 and g == 0):
                    dve.wait_ge(taken["attn_back"].sem, taken["attn_back"].at(j, g - 1))
                rows = bank("attn_back", g)[:, 0:NT * P].rearrange("p (t h d) -> p t h d", t=NT, h=G)
                V.reciprocal(rden[:, :, :], rows[:, :, :, DH]).then_inc(rden_made.sem, 1)
                dve.wait_ge(rden_made.sem, rden_made.at(j, g))
                V.tensor_tensor(attn[:, :, G * DH * g:G * DH * (g + 1)].rearrange("p t (h d) -> p t h d", h=G),
                                rows[:, :, :, 0:DH], rden[:, :, :].unsqueeze(3).to_broadcast([P, NT, G, DH]), ALU.mult
                                ).then_inc(taken["attn_back"].sem, 1)

            def add_to_rows(kind, b, t):
                dve.wait_ge(made[kind].sem, made[kind].at(b, t))
                row = h[:, bass.ds(b * NT + t, 1), :].rearrange("p a d -> p (a d)")
                V.tensor_tensor(row, bank(kind, t)[:, 0:D], row, ALU.add).then_inc(taken[kind].sem, 1)

            def take_scores(b):
                dve.wait_ge(made["router"].sem, made["router"].at(b))
                V.tensor_copy(scores8[:, bass.ds(b * NT, NT), :],
                              bank("router", 0)[:, 0:NT * E].rearrange("p (t e) -> p t e", t=NT)
                              ).then_inc(taken["router"].sem, 1)
                dve.wait_ge(taken["router"].sem, taken["router"].at(b))
                dve.sem_inc(dve_passed, 1)
                V.reduce_max(best[:, :], scores8[:, bass.ds(b * NT, NT), :], axis=AX.X).then_inc(best_found.sem, 1)

            def gate_rows(b):
                dve.wait_ge(gate_exp.sem, gate_exp.at(b))
                V.tensor_scalar(gate[:, :], gate[:, :], 1.0, None, ALU.add).then_inc(gate_step.sem, 1)
                dve.wait_ge(gate_step.sem, gate_step.at(b, 0))
                V.reciprocal(gate[:, :], gate[:, :]).then_inc(gate_step.sem, 1)
                dve.wait_ge(gate_step.sem, gate_step.at(b, 1))
                for t in range(NT):
                    V.tensor_scalar(xn2[:, t, :], xn2[:, t, :], gate[:, t:t + 1], None, ALU.mult
                                    ).then_inc(gated_made.sem, 1)

            def middle(b, f):
                n = FT[f]
                dve.wait_ge(tanh_made.sem, tanh_made.at(b, f))
                if not (isinstance(b, int) and b == 0 and f == 0):
                    dve.wait_ge(taken["up"].sem, taken["up"].at(b, f - 1))
                V.scalar_tensor_tensor(out=half_u[0:n, :], in0=tanh[0:n, f % 2, :], scalar=1.0,
                                       in1=bank("gate", f)[0:n, 0:TOK], op0=ALU.add, op1=ALU.mult
                                       ).then_inc(taken["gate"].sem, 1)
                dve.wait_ge(taken["gate"].sem, taken["gate"].at(b, f))
                dve.wait_ge(made["up"].sem, made["up"].at(b, f))
                dve.wait_ge(mid_low.sem, mid_low.at(b, f - 2) if f >= 2 else mid_low.at(b - 1))
                V.scalar_tensor_tensor(out=mid_f[0:n, f % 2, :], in0=half_u[0:n, :], scalar=0.5,
                                       in1=bank("up", f)[0:n, 0:TOK], op0=ALU.mult, op1=ALU.mult
                                       ).then_inc(taken["up"].sem, 1)

            pic_n = [0]

            def pic_step(ins):
                pic_n[0] += 1
                ins.then_inc(picture0_step, 1)
                dve.wait_ge(picture0_step, pic_n[0])

            dve.wait_ge(small_in, 32)
            V.tensor_scalar(taps[:, :, :], taps[:, :, :], 0.5, None, ALU.mult).then_inc(taps_halved, 1)
            dve.wait_ge(taps_halved, 1)
            dve.wait_ge(consts_made, CORE_CONSTS)
            dve.wait_ge(x_loaded.sem, x_loaded.at(0))
            middle_rows = gray[:, 1:3, 1:D + 1]
            pic_step(V.tensor_scalar(middle_rows, x_in[:, 0], GRAY[0], None, ALU.mult))
            for i in (1, 2):
                pic_step(V.scalar_tensor_tensor(out=middle_rows, in0=x_in[:, i], scalar=GRAY[i], in1=middle_rows,
                                                op0=ALU.mult, op1=ALU.add))
            split([w[:, :, :] for w in wqkv], as3(raw[0][:, 0:DC * 3 * D], DC), 0, 16)
            for n in range(2):
                for k in range(9):
                    if n == 0 and k == 0:
                        dve.wait_ge(halo_in.sem, halo_in.at(0))
                    if k == 0:
                        pic_step(V.tensor_scalar(edge[:, n], gray_rows(0), taps[:, n, 0:1], None, ALU.mult))
                    else:
                        pic_step(V.scalar_tensor_tensor(out=edge[:, n], in0=gray_rows(k), scalar=taps[:, n, k:k + 1],
                                                        in1=edge[:, n], op0=ALU.mult, op1=ALU.add))
            assert pic_n[0] == PICTURE0
            edges(0)
            split([w[:, :, :] for w in wo], as3(raw[1][:, 0:DC * D], DC), 1, 32)
            split([w[:, :, :] for w in wr], as3(raw[1][:, DC * D:DC * D + DC * E], DC), 1, 32)
            dve.wait_ge(text_in, 16 * NB)
            for n in range(4):
                dve.wait_ge(made["lora"].sem, n + 1)
                rows = h[:, 2 * NT * n + 2:2 * NT * n + 6:3, :]
                V.tensor_tensor(rows, bank("lora", n).rearrange("p (b d) -> p b d", b=2), rows, ALU.add
                                ).then_inc(taken["lora"].sem, 1)
            dve.wait_ge(edge_step.sem, edge_step.at(0))
            dve.wait_ge(taken["lora"].sem, 4)
            norm_stats(0, 0)
            norm_apply(0, 0, xn)
            for n in range(2):
                low_part("xT", n, 0, xT)
            for m in (0, 2, 1, 3):
                parts23(0, m)
            split([w[:, :, :] for w in wg], as3(raw[0][:, 0:DC * F], DC), 2, 16)
            split([w[:, :, :] for w in wu], as3(raw[1][:, 0:DC * F], DC), 3, 16)
            split([w[:, 0:NF - 1, :] for w in wd], as3(raw[0][:, 0:(NF - 1) * D], NF - 1), 4, 32)
            split([w[0:FT[-1], NF - 1, :] for w in wd], raw[0][0:FT[-1], (NF - 1) * D:NF * D], 4, 32)
            assert splits[0] == SPLITS
            for g in range(2):
                for i in range(12):
                    maxima(0, g, i)
                split_shift(0, g)
            edges(1)
            dve.wait_ge(edge_step.sem, edge_step.at(1))
            norm_stats(0, 1)
            norm_apply(0, 1, xn)

            def body(j, front, back, conv, end=False):
                f, b, c = j + 1, j - 1, j + 2
                for q in range(HALVES):
                    g, i = [(j, 2), (j, 3), (f, 0), (f, 1)][q // 6], 2 * (q % 6)
                    if not end and (q < 12 or front):
                        maxima(g[0], g[1], i)
                        maxima(g[0], g[1], i + 1)
                        if i == 10:
                            split_shift(*g)
                    for at_q, what, n, ahead in USES:
                        if at_q != q or not {1: front, 0: not end, -1: back}[ahead]:
                            continue
                        if what == "attn_back":
                            normalise(j + ahead, n)
                        elif what == "xT":
                            low_part("xT", n, f, xT)
                        elif what == "attnT":
                            low_part("attnT", n, b, attnT)
                        elif what == "qk":
                            parts23(f, n)
                        elif what == "proj":
                            add_to_rows("proj", b, n)
                        elif what == "x2T":
                            low_part("x2T", n, b, x2T)
                        elif what == "router":
                            take_scores(b)
                        elif what == "gate":
                            middle(b, n)
                            if n == 1:
                                gate_rows(b)
                        elif what == "down":
                            add_to_rows("down", b, n)
                    if q == 6 and back:
                        dve.wait_ge(taken["proj"].sem, taken["proj"].at(b))
                        norm_stats(1, b)
                    if q == 8 and back:
                        if not (isinstance(b, int) and b == 0):
                            dve.wait_ge(gated_out.sem, gated_out.at(b - 1))
                        norm_apply(1, b, xn2)
                    if q == 20 and conv:
                        edges(c)
                    if q == 21 and conv:
                        dve.wait_ge(edge_step.sem, edge_step.at(c))
                        norm_stats(0, c)
                    if q == 22 and conv:
                        norm_apply(0, c, xn)

            body(0, True, False, True)
            with dve.Fori(1, NB - 2) as j:
                body(j, True, True, True)
            body(NB - 2, True, True, False)
            body(NB - 1, False, True, False)
            body(NB, False, True, False, end=True)

            n_route = [0]

            def step(ins):
                n_route[0] += 1
                ins.then_inc(route_step, 1)
                dve.wait_ge(route_step, n_route[0])

            dve.wait_ge(consts_made, CONSTS)
            top = rt_small[:, 0:COLS]
            step(V.reduce_max(top, scores8[:, :, :], axis=AX.X))
            step(V.tensor_tensor(rt_a, scores8[:, :, :], top.unsqueeze(2).to_broadcast([P, COLS, E]), ALU.is_equal))
            iota_eb = iota_e[:, :].unsqueeze(1).to_broadcast([P, COLS, E])
            step(V.tensor_tensor(rt_a, rt_a, iota_eb, ALU.mult))
            step(V.tensor_reduce(top, rt_a, axis=AX.X, op=ALU.min))
            V.tensor_tensor(onehot, iota_eb, top.unsqueeze(2).to_broadcast([P, COLS, E]), ALU.is_equal
                            ).then_inc(onehot_made, 1)
            dve.wait_ge(rank_made, 1)
            count, tiles, base, last = (rt_small[:, 32 + 8 * i:40 + 8 * i] for i in range(4))
            step(V.tensor_copy(count, work[:, 1, 0:E]))
            step(V.tensor_tensor(rt_e24, count.unsqueeze(2).to_broadcast([P, E, COLS]),
                                 iota_k[:, :].unsqueeze(1).to_broadcast([P, E, COLS]), ALU.is_gt))
            step(V.tensor_reduce(tiles, rt_e24, axis=AX.X, op=ALU.add))
            step(V.tensor_tensor(rt_ee, lower_e[:, :, :], tiles.unsqueeze(1).to_broadcast([P, E, E]), ALU.mult))
            step(V.tensor_reduce(base, rt_ee, axis=AX.X, op=ALU.add))
            step(V.tensor_tensor(last, base, tiles, ALU.add))
            step(V.tensor_tensor(rt_te, iota_t[:, :].unsqueeze(2).to_broadcast([P, TILES, E]),
                                 last.unsqueeze(1).to_broadcast([P, TILES, E]), ALU.is_ge))
            expert, three = rt_b[:, 0:TILES], rt_b[:, 32:32 + TILES]
            step(V.tensor_reduce(expert, rt_te, axis=AX.X, op=ALU.add))
            step(V.tensor_scalar(expert, expert, float(E - 1), None, ALU.min))
            step(V.tensor_scalar(three, expert, 3.0, -3.0, ALU.is_ge, ALU.mult))
            step(V.tensor_tensor(rt_b[:, 64:64 + TILES], expert, three, ALU.add))
            step(V.tensor_scalar(three, expert, 6.0, -3.0, ALU.is_ge, ALU.mult))
            step(V.tensor_tensor(rt_b[:, 64:64 + TILES], rt_b[:, 64:64 + TILES], three, ALU.add))
            step(V.tensor_scalar(rt_b[:, 64:64 + TILES], rt_b[:, 64:64 + TILES], 1.0, None, ALU.mult))
            step(V.tensor_copy(route_i[0:1, 0:TILES], rt_b[0:1, 0:TILES]))
            step(V.tensor_copy(route_i[0:1, TILES:2 * TILES], rt_b[0:1, 64:64 + TILES]))
            step(V.tensor_scalar(route_i[0:1, 2 * TILES:2 * TILES + E], base[0:1, :], 1.0, None, ALU.max))
            step(V.scalar_tensor_tensor(out=rt_a, in0=base.unsqueeze(1).to_broadcast([P, COLS, E]), scalar=float(P),
                                        in1=work[:, 0, 0:COLS * E].rearrange("p (c e) -> p c e", c=COLS),
                                        op0=ALU.mult, op1=ALU.add))
            step(V.tensor_tensor(rt_a, rt_a, onehot, ALU.mult))
            step(V.tensor_reduce(top, rt_a, axis=AX.X, op=ALU.add))
            step(V.tensor_copy(rt_i[:, 0:COLS], top))
            step(V.tensor_scalar(rt_i[:, 32:32 + COLS], rt_i[:, 0:COLS], 7, None, ALU.arith_shift_right))
            step(V.tensor_scalar(rt_i[:, 0:COLS], rt_i[:, 0:COLS], P - 1, None, ALU.bitwise_and))
            within, tile = rt_b[:, 0:COLS], rt_b[:, 32:32 + COLS]
            step(V.tensor_copy(within, rt_i[:, 0:COLS]))
            step(V.tensor_copy(tile, rt_i[:, 32:32 + COLS]))
            tok = token[:, :, :].rearrange("p b t -> p (b t)")
            step(V.tensor_scalar(rt_i[:, 0:COLS], tok, 6, None, ALU.arith_shift_right))
            step(V.tensor_scalar(rt_i[:, 32:32 + COLS], tok, 63, None, ALU.bitwise_and))
            step(V.tensor_copy(rt_b[:, 64:64 + COLS], rt_i[:, 0:COLS]))
            step(V.tensor_copy(rt_b[:, 96:96 + COLS], rt_i[:, 32:32 + COLS]))
            step(V.tensor_tensor(tile_hot, iota_t[:, :].unsqueeze(1).to_broadcast([P, COLS, TILES]),
                                 tile.unsqueeze(2).to_broadcast([P, COLS, TILES]), ALU.is_equal))
            for i in range(2):
                V.tensor_tensor(tile_val[:, :, i, :], tile_hot,
                                rt_b[:, 64 + 32 * i:64 + 32 * i + COLS].unsqueeze(2).to_broadcast([P, COLS, TILES]),
                                ALU.mult).then_inc(slot_cols, 1)
            for c in range(COLS):
                if c >= 12:
                    dve.wait_ge(slots_read, c - 11)
                V.tensor_scalar(slot_hot[:, c % 12, :], iota_p[:, :], within[:, c:c + 1], None, ALU.is_equal
                                ).then_inc(slot_cols, 1)
            dve.wait_ge(slots_read, COLS)
            step(V.tensor_copy(rt_b[:, 0:TILES], work[:, 2, TILES:2 * TILES]))
            step(V.scalar_tensor_tensor(out=rt_b[:, 32:32 + TILES], in0=work[:, 2, 0:TILES], scalar=64.0,
                                        in1=rt_b[:, 0:TILES], op0=ALU.mult, op1=ALU.add))
            V.tensor_scalar(slot_of[:, :], rt_b[:, 32:32 + TILES], float(NTOK), None, ALU.add).then_inc(routed, 1)

            def e_middle(k):
                dve.wait_ge(e_tanh, k + 1)
                V.scalar_tensor_tensor(out=u_e, in0=tanh_e, scalar=1.0, in1=st_ps[:, :, 0:HF],
                                       op0=ALU.add, op1=ALU.mult).then_inc(e_u, 1)
                dve.wait_ge(e_u, k + 1)
                if not (isinstance(k, int) and k == 0):
                    dve.wait_ge(e_midT, k)
                dve.wait_ge(e_up, k + 1)
                V.scalar_tensor_tensor(out=mid_e, in0=u_e, scalar=0.5, in1=sm_ps[:, :, 0:HF],
                                       op0=ALU.mult, op1=ALU.mult).then_inc(e_mid, 1)

            def e_mid_transposed(k):
                dve.wait_ge(e_midT, k + 1)
                if not (isinstance(k, int) and k == 0):
                    dve.wait_ge(e_down, k)
                V.tensor_copy(midT_e[:, 4 * P:5 * P], work[:, 1, 0:P]).then_inc(e_midT_b, 1)
                V.tensor_copy(midT_e[0:FT[-1], 5 * P:6 * P], work[0:FT[-1], 1, P:2 * P]).then_inc(e_midT_b, 1)

            e_middle(0)
            with dve.Fori(1, TILES) as k:
                e_mid_transposed(k - 1)
                e_middle(k)
            e_mid_transposed(TILES - 1)

        @block.tensor
        def _(pe):
            MM = nc.tensor.matmul

            def three_passes(out_, pairs):
                terms = [(a[i], b[k]) for a, b in pairs for i, k in ((0, 0), (0, 1), (1, 0))]
                for n, (a, b) in enumerate(terms):
                    last = MM(out_, a, b, start=(n == 0), stop=(n == len(terms) - 1))
                return last

            def transposes(phase, j, kind, n, b, src, c):
                wait_bank(pe, phase, j, kind, n)
                for t in range(NT):
                    last = nc.tensor.transpose(bank(kind, n)[:, t * P:(t + 1) * P], src[:, t, c * P:(c + 1) * P],
                                               ident[:, :])
                last.then_inc(made[kind].sem, 1)

            def project_qk(phase, j, b, m):
                wait_bank(pe, phase, j, "qk", m)
                pe.wait_ge(taken["xT"].sem, taken["xT"].at(b))
                three_passes(bank("qk", m)[:, 0:TOK],
                             [([w[:, c, m * P:(m + 1) * P] for w in wqkv], [a[:, c, :] for a in xT]) for c in range(DC)]
                             ).then_inc(made["qk"].sem, 1)

            def project_v(phase, j, b, t):
                wait_bank(pe, phase, j, "v", t)
                three_passes(bank("v", t)[:, 0:D],
                             [([a[:, c, t * P:(t + 1) * P] for a in xT], [w[:, c, 2 * D:3 * D] for w in wqkv])
                              for c in range(DC)]).then_inc(made["v"].sem, 1)

            def search_scores(b, g, i):
                hh, t = divmod(i, NT)
                n = 12 * g + i
                if i == 0:
                    pe.wait_ge(stack_in[g].sem, stack_in[g].at(b))
                if not (isinstance(b, int) and b == 0 and n < 2):
                    pe.wait_ge(smax_found.sem, smax_found.at(b, n - 2))
                MM(sm_ps[:, n % 2, 0:TOK], q_st[0:KROWS, G * g + hh, t * P:(t + 1) * P], k_st[0:KROWS, G * g + hh, :],
                   start=True, stop=True).then_inc(smax_made.sem, 1)

            def transpose_shift(phase, j, b, g):
                wait_bank(pe, phase, j, "shift", g)
                pe.wait_ge(shift_split.sem, shift_split.at(b, g))
                dst = bank("shift", g).bitcast(BF16)
                for t in range(NT):
                    last = nc.tensor.transpose(dst[0:3 * G, t * P:(t + 1) * P],
                                               shift_p[:, t, :, :].rearrange("p a h -> p (a h)"), identb[:, :])
                last.then_inc(made["shift"].sem, 1)

            def scores(j, step, half):
                g, kc = divmod(step, NT)
                if kc == 0 and half == 0:
                    pe.wait_ge(shift_in[g].sem, shift_in[g].at(j))
                for hh in (2 * half, 2 * half + 1):
                    n = 4 * step + hh
                    if not (isinstance(j, int) and j == 0 and n < 2):
                        pe.wait_ge(exp_made.sem, exp_made.at(j, n - 2))
                    MM(st_ps[:, hh % 2, 0:TOK], k_st[0:KROWS + 3, G * g + hh, kc * P:(kc + 1) * P],
                       q_st[0:KROWS + 3, G * g + hh, :], start=True, stop=True).then_inc(st_made.sem, 1)

            def weigh_values(j, step):
                g, kc = divmod(step, NT)
                if step == 0:
                    pe.wait_ge(taken["v"].sem, taken["v"].at(j))
                if kc == 0 and not (isinstance(j, int) and j == 0 and g == 0):
                    pe.wait_ge(ot_copied.sem, ot_copied.at(j, g - 1))
                pe.wait_ge(exp_made.sem, exp_made.at(j, 4 * step + 3))
                for hh in range(G):
                    last = MM(pv_ps[2 * DH * hh:2 * DH * (hh + 1), 0:TOK], v_sb[:, kc, G * g + hh, :],
                              probs[:, step % 3, hh, :], start=(kc == 0), stop=(kc == NT - 1))
                last.then_inc(pv_made.sem, 1)

            def transpose_back(phase, j, b, g):
                wait_bank(pe, phase, j, "attn_back", g)
                pe.wait_ge(ot_copied.sem, ot_copied.at(b, g))
                for t in range(NT):
                    last = nc.tensor.transpose(bank("attn_back", g)[:, t * P:(t + 1) * P], ot[:, t * P:(t + 1) * P],
                                               ident[:, :])
                last.then_inc(made["attn_back"].sem, 1)

            def project_out(phase, j, b, t):
                wait_bank(pe, phase, j, "proj", t)
                pe.wait_ge(taken["attnT"].sem, taken["attnT"].at(b))
                three_passes(bank("proj", t)[:, 0:D],
                             [([a[:, c, t * P:(t + 1) * P] for a in attnT], [w[:, c, :] for w in wo])
                              for c in range(DC)]).then_inc(made["proj"].sem, 1)

            def router_scores(phase, j, b):
                wait_bank(pe, phase, j, "router", 0)
                pe.wait_ge(taken["x2T"].sem, taken["x2T"].at(b))
                for t in range(NT):
                    last = three_passes(bank("router", 0)[:, t * E:(t + 1) * E],
                                        [([a[:, c, t * P:(t + 1) * P] for a in x2T], [w[:, c, :] for w in wr])
                                         for c in range(DC)])
                last.then_inc(made["router"].sem, 1)

            def shared_up(phase, j, b, f, kind, w):
                wait_bank(pe, phase, j, kind, f)
                three_passes(bank(kind, f)[0:FT[f], 0:TOK],
                             [([a[:, c, f * P:f * P + FT[f]] for a in w], [a[:, c, :] for a in x2T])
                              for c in range(DC)]).then_inc(made[kind].sem, 1)

            def shared_down(phase, j, b, t):
                wait_bank(pe, phase, j, "down", t)
                pe.wait_ge(mid_low.sem, mid_low.at(b))
                three_passes(bank("down", t)[:, 0:D],
                             [([a[0:FT[f], f, t * P:(t + 1) * P] for a in mid], [w[0:FT[f], f, :] for w in wd])
                              for f in range(NF)]).then_inc(made["down"].sem, 1)

            pe.wait_ge(consts_made, CORE_CONSTS)
            pe.wait_ge(lora_in, 16 * NB)
            pe.wait_ge(small_in, 32)
            for n in range(2):
                for i in range(4):
                    last = nc.tensor.transpose(bank("loraT", n)[0:RANK, i * P:(i + 1) * P], lora_a[:, 4 * n + i, :],
                                               ident[:, :])
                last.then_inc(made["loraT"].sem, 1)
            for n in range(4):
                if n == 0:
                    pe.wait_ge(taken["loraT"].sem, 2)
                wait_bank(pe, "prologue", -1, "lora", n)
                for i in range(2):
                    bt = 2 * n + i
                    last = MM(bank("lora", n)[:, i * D:(i + 1) * D], lora_aT[:, bt * P:(bt + 1) * P], lora_b,
                              start=True, stop=True)
                last.then_inc(made["lora"].sem, 1)
            pe.wait_ge(w_split, 1)
            pe.wait_ge(ln_done[0].sem, ln_done[0].at(0))
            for c in range(DC):
                transposes("prologue", -1, "xT", c, 0, xn, c)
            for m in (0, 2, 1, 3):
                project_qk("prologue", -1, 0, m)
            for i in range(12):
                search_scores(0, 0, i)
            transpose_shift("prologue", -1, 0, 0)
            for i in range(12):
                search_scores(0, 1, i)
            for t in range(NT):
                project_v("prologue", -1, 0, t)
            pe.wait_ge(w_split, SPLITS)

            def body(phase, j, front, back, end=False):
                f, b = j + 1, j - 1
                for q in range(HALVES + 1):
                    tail = q == HALVES
                    if not end and not tail:
                        scores(j, q // 2, q % 2)
                    if not end and q in (6, 12, 18):
                        weigh_values(j, q // 2 - 1)
                    if not end and tail:
                        weigh_values(j, 11)
                    if not end and not tail and (q < 12 or front):
                        bb, g = [(j, 2), (j, 3), (f, 0), (f, 1)][q // 6]
                        search_scores(bb, g, 2 * (q % 6))
                        search_scores(bb, g, 2 * (q % 6) + 1)
                    for at_q, what, n, ahead in USES:
                        if at_q != q or not {1: front, 0: not end, -1: back}[ahead]:
                            continue
                        if what == "attn_back":
                            transpose_back(phase, j, j + ahead, n)
                        elif what == "shift":
                            transpose_shift(phase, j, j + ahead, n)
                        elif what == "xT":
                            pe.wait_ge(ln_done[0].sem, ln_done[0].at(f))
                            transposes(phase, j, "xT", n, f, xn, n)
                        elif what == "attnT":
                            pe.wait_ge(taken["attn_back"].sem, taken["attn_back"].at(b))
                            transposes(phase, j, "attnT", n, b, attn, n)
                        elif what == "x2T":
                            pe.wait_ge(ln_done[1].sem, ln_done[1].at(b))
                            transposes(phase, j, "x2T", n, b, xn2, n)
                        elif what == "qk":
                            project_qk(phase, j, f, n)
                        elif what == "v":
                            project_v(phase, j, f, n)
                        elif what == "proj":
                            project_out(phase, j, b, n)
                        elif what == "router":
                            router_scores(phase, j, b)
                        elif what == "gate":
                            shared_up(phase, j, b, n, "gate", wg)
                        elif what == "up":
                            shared_up(phase, j, b, n, "up", wu)
                        elif what == "down":
                            shared_down(phase, j, b, n)
                    if not end and q % 2 == 1 and q % 6 != 1:
                        weigh_values(j, q // 2 - 1)

            body(0, 0, True, False)
            with pe.Fori(1, NB - 2) as j:
                body("loop", j, True, True)
            body(NB - 2, NB - 2, True, True)
            body(NB - 1, NB - 1, False, True)
            body("end", NB, False, True, end=True)

            pe.wait_ge(onehot_made, 1)
            hot = onehot.rearrange("p c e -> p (c e)")
            MM(work[:, 0, 0:COLS * E], before[:, :], hot, start=True, stop=False)
            for c in range(1, COLS):
                MM(work[:, 0, c * E:COLS * E], onesb[:, :], hot[:, 0:(COLS - c) * E], start=False, stop=(c == COLS - 1))
            for c in range(COLS):
                last = MM(work[:, 1, 0:E], onesb[:, :], hot[:, c * E:(c + 1) * E], start=(c == 0), stop=(c == COLS - 1))
            last.then_inc(rank_made, 1)
            for c in range(COLS):
                pe.wait_ge(slot_cols, 2 + c + 1)
                MM(work[:, 2, 0:2 * TILES], slot_hot[:, c % 12, :], tile_val[:, c].rearrange("p i t -> p (i t)"),
                   start=(c == 0), stop=(c == COLS - 1)).then_inc(slots_read, 1)
            pe.wait_ge(routed, 1)

            def e_transpose(k, i, arrived):
                pe.wait_ge(row_in[i], arrived)
                if not (isinstance(k, int) and k == 0):
                    pe.wait_ge(e_xT_copied, k)
                for c in range(DC):
                    last = nc.tensor.transpose(pv_ps[:, c * P:(c + 1) * P], xg[:, i, c * P:(c + 1) * P], ident[:, :])
                last.then_inc(e_xT, 1)

            def e_gate_products(k):
                expert = pe.value_load(route_i[0:1, bass.ds(k, 1)], min_val=0, max_val=E - 1)
                place = pe.value_load(route_i[0:1, bass.ds(k + TILES, 1)], min_val=0, max_val=2)
                pe.wait_ge(expert_ready, expert + 1)
                pe.wait_ge(e_xT_copied, k + 1)
                if not (isinstance(k, int) and k == 0):
                    pe.wait_ge(e_u, k)
                e_wide(wx[0], st_ps, place).then_inc(e_gate_made, 1)
                return place

            def e_up_products(k, place):
                if not (isinstance(k, int) and k == 0):
                    pe.wait_ge(e_mid, k)
                e_wide(wx[1], sm_ps, place).then_inc(e_up, 1)

            def e_wide(w, dst, place):
                for half in range(2):
                    for c in range(DC):
                        last = MM(dst[:, half, 0:HF], xT_e[:, c * P:(c + 1) * P],
                                  w[:, bass.ds(place, 1), c, half * HF:(half + 1) * HF].rearrange("p a w -> p (a w)"),
                                  start=(c == 0), stop=(c == DC - 1))
                return last

            def e_transpose_mid(k):
                pe.wait_ge(e_mid, k + 1)
                if not (isinstance(k, int) and k == 0):
                    pe.wait_ge(e_midT_a, k)
                    pe.wait_ge(e_midT_b, 2 * k)
                for f in range(NF):
                    last = nc.tensor.transpose(work[0:FT[f], f // 4, (f % 4) * P:(f % 4 + 1) * P],
                                               mid_row[:, f * P:f * P + FT[f]], ident[:, :])
                last.then_inc(e_midT, 1)

            def e_down_products(k):
                place = pe.value_load(route_i[0:1, bass.ds(k + TILES, 1)], min_val=0, max_val=2)
                pe.wait_ge(e_midT_a, k + 1)
                pe.wait_ge(e_midT_b, 2 * k + 2)
                if not (isinstance(k, int) and k == 0):
                    pe.wait_ge(e_y, k)
                for f in range(NF):
                    last = MM(work[:, 2, 0:D], midT_e[0:FT[f], f * P:(f + 1) * P],
                              wx[2][0:FT[f], bass.ds(place, 1), f, :].rearrange("p a w -> p (a w)"),
                              start=(f == 0), stop=(f == NF - 1))
                last.then_inc(e_down, 1)

            def e_turn(k, i, arrived):
                place = e_gate_products(k)
                e_transpose_mid(k - 1)
                e_up_products(k, place)
                if arrived is not None:
                    e_transpose(k + 1, i, arrived)
                e_down_products(k - 1)

            e_transpose(0, 0, 16)
            e_up_products(0, e_gate_products(0))
            e_transpose(1, 1, 16)
            with pe.Fori(1, TILES - 2, 2) as k:
                e_turn(k, 0, 8 * k + 24)
                e_turn(k + 1, 1, 8 * k + 24)
            e_turn(TILES - 2, 0, 16 * ((TILES - 1) // 2 + 1))
            e_turn(TILES - 1, 1, None)
            e_transpose_mid(TILES - 1)
            e_down_products(TILES - 1)


def kernel(**inputs):
    import numpy as _np
    import concourse.bacc as _bacc
    from concourse import mybir as _mybir
    from concourse.bass_utils import run_bass_kernel_spmd as _run

    t = {k: _np.asarray(v) for k, v in inputs.items()}
    laid = {
        "x": t["x"], "x_txt": t["x_txt"], "scharr": t["L0_tok_scharr"],
        "base_rows": t["L0_txt_base_weight"].T, "lora_A": t["L0_txt_lora_A"], "lora_B": t["L0_txt_lora_B"],
        "w_qkvT": t["L0_attn_w_qkv"].T, "w_outT": t["L0_attn_w_out"].T, "router": t["L0_ffn_router_DE"],
        "w1": t["L0_ffn_w1_eDF"], "w3": t["L0_ffn_w3_eDF"], "w2": t["L0_ffn_w2_eFD"],
        "ws1": t["L0_ffn_ws1_DF"], "ws3": t["L0_ffn_ws3_DF"], "ws2": t["L0_ffn_ws2_FD"],
    }
    nc = _bacc.Bacc("TRN2", target_bir_lowering=False, num_devices=1)
    arrays, args = {}, []
    for name, a in laid.items():
        a = _np.ascontiguousarray(a)
        arrays[f"in_{name}_dram"] = a
        args.append(nc.dram_tensor(f"in_{name}_dram", a.shape, _mybir.dt.from_np(a.dtype), kind="ExternalInput").ap())
    shape = (t["x"].shape[0], t["x"].shape[2] + t["x_txt"].shape[1], t["x"].shape[3])
    args.append(nc.dram_tensor("out_0_dram", shape, _mybir.dt.float32, kind="ExternalOutput").ap())
    embed_block_moe_kernel(nc, *args)
    r = _run(nc, [arrays], core_ids=[0])
    return r.results[0]["out_0_dram"]
```

```python
from contextlib import ExitStack

import concourse.bass as bass
from concourse import mybir

ALU = mybir.AluOpType
ACT = mybir.ActivationFunctionType
AX = mybir.AxisListType
F32 = mybir.dt.float32
F32R = mybir.dt.float32r
BF16 = mybir.dt.bfloat16
I32 = mybir.dt.int32

P = 128
EPS = 1e-5
GRAY = (0.2989, 0.587, 0.114)

USES = [
    (0, "attn_back", 3, -1), (0, "shift", 1, 0),
    (1, "xT", 0, 1), (1, "xT", 1, 1),
    (2, "attnT", 0, -1), (2, "attnT", 1, -1),
    (3, "qk", 0, 1),
    (4, "qk", 2, 1), (4, "proj", 0, -1),
    (5, "proj", 1, -1), (5, "proj", 2, -1),
    (6, "shift", 2, 0),
    (7, "qk", 1, 1),
    (8, "attn_back", 0, 0), (8, "x2T", 0, -1), (8, "x2T", 1, -1),
    (9, "router", 0, -1), (9, "qk", 3, 1),
    (10, "gate", 0, -1),
    (11, "up", 0, -1),
    (12, "shift", 3, 0), (12, "gate", 1, -1),
    (13, "up", 1, -1), (13, "gate", 2, -1),
    (14, "attn_back", 1, 0), (14, "up", 2, -1),
    (15, "gate", 3, -1), (15, "up", 3, -1),
    (16, "gate", 4, -1),
    (17, "up", 4, -1), (17, "gate", 5, -1),
    (18, "shift", 0, 1), (18, "up", 5, -1),
    (19, "down", 0, -1),
    (20, "attn_back", 2, 0),
    (21, "down", 1, -1),
    (23, "down", 2, -1),
    (24, "v", 0, 1), (24, "v", 1, 1), (24, "v", 2, 1),
]
BANK = {(what, n): i % 3 for i, (_, what, n, _) in enumerate(USES)}
PROLOGUE = [("loraT", 0), ("loraT", 1), ("lora", 0), ("lora", 1), ("lora", 2), ("lora", 3),
            ("xT", 0), ("xT", 1), ("qk", 0), ("qk", 2), ("qk", 1), ("qk", 3), ("shift", 0),
            ("v", 0), ("v", 1), ("v", 2)]
for _i, _u in enumerate(PROLOGUE[:6]):
    BANK[_u] = _i % 3
PLACE = {("qk", 0): 0, ("qk", 2): 1, ("qk", 1): 2, ("qk", 3): 3}
HALVES = 24


class Signal:

    def __init__(self, sem, per, by=1):
        self.sem, self.per, self.by = sem, per, by

    def at(self, batch, n=None):
        return (batch * self.per + (self.per if n is None else n + 1)) * self.by


def embed_block_moe_kernel(nc, x, x_txt, scharr, base_rows, lora_A, lora_B, w_qkvT, w_outT, router,
                           w1, w3, w2, ws1, ws3, ws2, out):
    NB, C, IMG, D = x.shape
    TXT = x_txt.shape[1]
    TOK = IMG + TXT
    NT = TOK // P
    HEADS = 16
    DH = D // HEADS
    VOCAB, RANK = lora_A.shape
    E, _, F = w1.shape
    NF = (F + P - 1) // P
    FT = [min(P, F - P * f) for f in range(NF)]
    DC = D // P
    G = 4
    NG = HEADS // G
    NTOK = NB * TOK
    COLS = NB * NT
    TILES = NTOK // P + E - 1
    HF = F // 2
    PARTS = [(0, 0), (0, 1), (0, 2), (1, 0), (1, 1), (2, 0)]
    KROWS = len(PARTS) * DH
    assert TILES % 2 == 1 and NT == 3 and DC == 2 and DH == 16 and KROWS + 3 <= P and HF <= 512 and HF % 2 == 0

    parts_dram = nc.dram_tensor("parts_dram", [3, 4, P, TOK], BF16).ap()
    shift_dram = nc.dram_tensor("shift_dram", [3, HEADS, TOK], BF16).ap()
    gated_dram = nc.dram_tensor("gated_dram", [NB, TOK, D], F32).ap()

    ctx = ExitStack()
    with ctx:
        def sb(name, shape, dt, scope=ctx):
            return scope.enter_context(nc.sbuf_tensor(name, shape, dt))

        def ps(name, shape, dt):
            return ctx.enter_context(nc.psum_tensor(name, shape, dt))

        def signal(name, per, by=1):
            return Signal(ctx.enter_context(nc.semaphore(name)), per, by)

        def sem(name):
            return ctx.enter_context(nc.semaphore(name))

        st_ps = ps("st_ps", [P, 2, 512], F32)
        sm_ps = ps("sm_ps", [P, 2, 512], F32)
        pv_ps = ps("pv_ps", [P, 512], F32)
        work = ps("work", [P, 3, 512], F32)

        ident = sb("ident", [P, P], F32)
        identb = sb("identb", [P, P], BF16)
        before = sb("before", [P, P], BF16)
        onesb = sb("onesb", [P, P], BF16)
        iota_p = sb("iota_p", [P, P], F32)
        iota_t = sb("iota_t", [P, TILES], F32)
        iota_e = sb("iota_e", [P, E], F32)
        iota_k = sb("iota_k", [P, COLS], F32)
        lower_e = sb("lower_e", [P, E, E], F32)
        token = sb("token", [P, NB, NT], I32)
        scores8 = sb("scores8", [P, COLS, E], F32)
        slot_of = sb("slot_of", [P, TILES], I32)
        route_i = sb("route_i", [1, 2 * TILES + E], I32)
        arena = sb("arena", [P, 14592], F32)
        at = [0]

        def room(words):
            at[0] += words
            return arena[:, at[0] - words:at[0]]

        q_st = room(HEADS * TOK // 2).bitcast(BF16).rearrange("p (h t) -> p h t", h=HEADS)
        k_st = room(HEADS * TOK // 2).bitcast(BF16).rearrange("p (h t) -> p h t", h=HEADS)
        parts = room(6 * TOK).bitcast(BF16).rearrange("p (a m t) -> p a m t", a=3, m=4)
        v_sb = room(NT * HEADS * 2 * DH).rearrange("p (t h d) -> p t h d", t=NT, h=HEADS)
        probs_room = room(3 * G * TOK)
        probs = probs_room.rearrange("p (s g t) -> p s g t", s=3, g=G)
        at[0] = 0
        wx = [room(3 * n * w).rearrange("p (s c w) -> p s c w", s=3, c=n) for n, w in ((DC, F), (DC, F), (NF, D))]
        raw = [probs_room[:, i * NF * D:(i + 1) * NF * D] for i in range(2)]
        text_room = probs_room[:, 2 * NF * D:3 * NF * D]
        lora_a = text_room[:, 0:NB * RANK].rearrange("p (b r) -> p b r", b=NB)
        lora_b = text_room[0:RANK, NB * RANK:NB * RANK + D]
        lora_aT = text_room[0:RANK, NB * RANK + D:NB * RANK + D + NB * P]
        x_in = sb("x_in", [P, C, 2, D], F32)
        product = sb("product", [P, 2, 2, D], F32)
        gray = sb("gray", [P, 4, D + 2], F32)
        edge = sb("edge", [P, 2, 2, D], F32)
        taps = sb("taps", [P, 2, 9], F32)
        h = sb("h", [P, COLS, D], F32)
        xn = sb("xn", [P, NT, D], F32)
        xn2 = sb("xn2", [P, NT, D], F32)
        xT = [sb(f"xT_{s}", [P, DC, TOK], F32R) for s in ("high", "low")]
        attnT = [sb(f"attnT_{s}", [P, DC, TOK], F32R) for s in ("high", "low")]
        x2T = attnT
        mid = [sb(f"mid_{s}", [P, NF, TOK], F32R) for s in ("high", "low")]
        mid_f = sb("mid_f", [P, 2, TOK], F32)
        tanh = sb("tanh", [P, 2, TOK], F32)
        half_u = sb("half_u", [P, TOK], F32)
        rest = sb("rest", [P, 2, TOK], F32)
        attn = sb("attn", [P, NT, D], F32)
        ot = sb("ot", [P, TOK], F32)
        stats = sb("stats", [P, 2, NT, 6], F32)
        mv = sb("mv", [P, 2, NT, 2], F32)
        rstd = sb("rstd", [P, 2, NT], F32)
        smax = sb("smax", [P, NT, G], F32)
        smax_r = sb("smax_r", [P, NT, G], F32)
        shift_p = sb("shift_p", [P, NT, 3, G], BF16)
        shift_T = sb("shift_T", [3 * G, TOK], BF16)
        rden = sb("rden", [P, NT, G], F32)
        best = sb("best", [P, NT], F32)
        gate = sb("gate", [P, NT], F32)
        wqkv = [sb(f"wqkv_{s}", [P, DC, 3 * D], F32R) for s in ("high", "low")]
        wo = [sb(f"wo_{s}", [P, DC, D], F32R) for s in ("high", "low")]
        wr = [sb(f"wr_{s}", [P, DC, E], F32R) for s in ("high", "low")]
        wg = [sb(f"wg_{s}", [P, DC, F], F32R) for s in ("high", "low")]
        wu = [sb(f"wu_{s}", [P, DC, F], F32R) for s in ("high", "low")]
        wd = [sb(f"wd_{s}", [P, NF, D], F32R) for s in ("high", "low")]
        ids = sb("ids", [P, NB], I32)
        ids_n = sb("ids_n", [P, NB], I32)

        consts_made = sem("consts_made")
        sp_passed, pool_passed, dve_passed, pe_passed = (sem(f"{e}_passed") for e in ("sp", "pool", "dve", "pe"))
        small_in = sem("small_in")
        weights_in = [sem(f"weights_in{i}") for i in range(6)]
        ids_step = sem("ids_step")
        text_in = sem("text_in")
        lora_in = sem("lora_in")
        w_high = sem("w_high")
        w_split = sem("w_split")
        x_loaded = signal("x_loaded", 1, 16)
        picture0_step = sem("picture0_step")
        gray_begun = signal("gray_begun", 1)
        product_made = signal("product_made", 18)
        product_added = signal("product_added", 18)
        halo_in = signal("halo_in", 2, 16)
        first_tap = signal("first_tap", 2)
        edge_step = signal("edge_step", 3)
        ln_stats = [signal(f"ln{i}_stats", 3) for i in (1, 2)]
        ln_aggr = [signal(f"ln{i}_aggr", 3) for i in (1, 2)]
        ln_rstd = [signal(f"ln{i}_rstd", 2) for i in (1, 2)]
        ln_done = [signal(f"ln{i}_done", 3) for i in (1, 2)]
        KINDS = {"attn_back": 4, "shift": 4, "xT": 2, "attnT": 2, "qk": 4, "proj": 3, "x2T": 2,
                 "router": 1, "gate": 6, "up": 6, "down": 3, "v": 3, "loraT": 2, "lora": 4}
        made = {k: signal(f"{k}_made", n) for k, n in KINDS.items()}
        taken = {k: signal(f"{k}_taken", n) for k, n in KINDS.items()}
        high = {k: signal(f"{k}_high", KINDS[k]) for k in ("xT", "attnT", "x2T", "qk")}
        tanh_made = signal("tanh_made", 6)
        mid_high = signal("mid_high", 6)
        mid_low = signal("mid_low", 6)
        part2_made = signal("part2_made", 4)
        parts_made = signal("parts_made", 4)
        parts_out = signal("parts_out", 4, 16)
        stack_in = [signal(f"stack_in{g}", 12, 16) for g in range(NG)]
        smax_made = signal("smax_made", 12 * NG)
        smax_found = signal("smax_found", 12 * NG)
        shift_step = signal("shift_step", 3 * NG)
        shift_split = signal("shift_split", NG)
        shift_out = signal("shift_out", NG, 16)
        shift_in = [signal(f"shift_in{g}", 3, 16) for g in range(NG)]
        st_made = signal("st_made", 12 * NG)
        exp_made = signal("exp_made", 12 * NG)
        pv_made = signal("pv_made", 12)
        ot_copied = signal("ot_copied", 4)
        rden_made = signal("rden_made", 4)
        router_made = signal("router_scores_made", 1)
        router_copied = signal("router_copied", 1)
        best_found = signal("best_found", 1)
        gate_exp = signal("gate_exp", 1)
        gate_step = signal("gate_step", 2)
        gated_made = signal("gated_made", 3)
        gated_out = signal("gated_out", 2, 16)
        rows_out = signal("rows_out", 2, 16)
        route_step = sem("route_step")
        routed = sem("routed")
        rank_made = sem("rank_made")
        slots_made = sem("slots_made")
        expert_in = [sem(f"expert_in{i}") for i in range(2)]
        expert_ready = sem("expert_ready")
        row_in = [sem(f"row_in{i}") for i in range(2)]
        row_cleared = sem("row_cleared")
        e_xT = sem("e_xT")
        e_xT_copied = sem("e_xT_copied")
        e_gate_made = sem("e_gate_made")
        e_up = sem("e_up")
        e_tanh = sem("e_tanh")
        e_u = sem("e_u")
        e_mid = sem("e_mid")
        e_midT = sem("e_midT")
        e_midT_a = sem("e_midT_a")
        e_midT_b = sem("e_midT_b")
        e_down = sem("e_down")
        e_y = sem("e_y")
        row_out = [sem(f"row_out{i}") for i in range(2)]

        x_room = x_in[:, :, :, :].rearrange("p c r w -> p (c r w)")
        xg = x_room[:, 0:2 * D].rearrange("p (i d) -> p i d", i=2)
        y_e = x_room[:, 2 * D:4 * D].rearrange("p (i d) -> p i d", i=2)
        xT_e = x_room[:, 4 * D:5 * D]
        tanh_e = gray[:, :, :].rearrange("p r w -> p (r w)")[:, 0:F].rearrange("p (i n) -> p i n", i=2)
        u_e = edge[:, :, :, :].rearrange("p f r w -> p (f r w)")[:, 0:F].rearrange("p (i n) -> p i n", i=2)
        mid_row = xn[:, :, :].rearrange("p t d -> p (t d)")[:, 0:F]
        mid_e = mid_row.rearrange("p (i n) -> p i n", i=2)
        midT_e = xn2[:, :, :].rearrange("p t d -> p (t d)")
        t_room = product[:, :, :, :].rearrange("p i r w -> p (i r w)")
        rt_a = t_room[:, 0:COLS * E].rearrange("p (c e) -> p c e", c=COLS)
        rt_e24 = t_room[:, COLS * E:2 * COLS * E].rearrange("p (e c) -> p e c", e=E)
        rt_te = t_room[:, 2 * COLS * E:2 * COLS * E + TILES * E].rearrange("p (t e) -> p t e", t=TILES)
        rt_ee = t_room[:, 640:640 + E * E].rearrange("p (e c) -> p e c", e=E)
        rt_b = t_room[:, 704:704 + P]
        rt_small = t_room[:, 832:896]
        rt_i = t_room[:, 896:960].bitcast(I32)
        onehot = gray[:, 0, 0:COLS * E // 2].bitcast(BF16).rearrange("p (c e) -> p c e", c=COLS)
        tile_hot = attn[:, :, :].rearrange("p t d -> p (t d)")[:, 0:COLS * TILES].rearrange("p (c t) -> p c t", c=COLS)
        tile_val = edge[:, :, :, :].rearrange("p f r w -> p (f r w)")[:, 0:COLS * TILES].bitcast(BF16)\
            .rearrange("p (c i t) -> p c i t", c=COLS, i=2)
        slot_hot = xn[:, :, :].rearrange("p t d -> p (t d)").bitcast(BF16).rearrange("p (c s) -> p c s", c=12)
        slot_i = sb("slot_i", [P, 4], I32)
        minus_half = sb("minus_half", [P, NT], F32)
        router_T = half_u[0:E, :]
        gated_rows = gated_dram.rearrange("b t d -> (b t) d")
        out_rows = out.rearrange("b t d -> (b t) d")
        ids_in = sem("ids_in")
        taps_halved = sem("taps_halved")
        onehot_made = sem("onehot_made")
        slot_cols = sem("slot_cols")
        slots_read = sem("slots_read")
        slot_picked = sem("slot_picked")
        CONSTS, CORE_CONSTS, FIRST_CONSTS, SPLITS, PICTURE0 = 18, 10, 8, 7, 21
        PRODUCT_AT = [1, 2] + [n + 3 if n < 10 else n + 2 for n in range(2, 18)]
        SPLIT_AT = {q + 1: f for q, what, f, _ in USES if what == "up"}

        def gray_rows(k):
            dy, dx = divmod(k, 3)
            return gray[:, dy:dy + 2, dx:dx + D]

        def uses_of(phase):
            if phase == "prologue":
                return [(None, what, n, 1) for what, n in PROLOGUE]
            front, back, core_ = phase != NB - 1 and phase != "end", phase != 0, phase != "end"
            return [u for u in USES if {1: front, 0: core_, -1: back}[u[3]]]

        def phase_before(phase):
            return {"prologue": None, 0: "prologue", "loop": "loop", NB - 2: "loop",
                    NB - 1: NB - 2, "end": NB - 1}[phase]

        def wait_bank(pe, phase, j, what, n):
            seq = uses_of(phase)
            at = [(u[1], u[2]) for u in seq].index((what, n))
            back = 0
            while True:
                at -= 1
                if at < 0:
                    phase, back = phase_before(phase), back + 1
                    if phase is None:
                        return
                    seq = uses_of(phase)
                    at = len(seq) - 1
                if BANK[seq[at][1], seq[at][2]] == BANK[what, n]:
                    break
            _, kind, m, ahead = seq[at]
            batch = 0 if kind in ("lora", "loraT") else j - back + ahead
            pe.wait_ge(taken[kind].sem, taken[kind].at(batch, PLACE.get((kind, m), m)))

        def bank(what, n):
            return work[:, BANK[what, n], :]

        def head_rows(g):
            return g // 2, (g % 2) * G * DH

        block = ctx.enter_context(nc.Block())

        @block.sync
        def _(sp):
            def load_x(b):
                if isinstance(b, int) and b == 1:
                    sp.wait_ge(picture0_step, 3)
                elif not isinstance(b, int) or b > 1:
                    sp.wait_ge(product_made.sem, product_made.at(b - 2, 1))
                sp.dma_start(x_in[:, :, :, :].rearrange("p c r w -> p c (r w)"),
                             x[bass.ds(b, 1)].rearrange("a c (p r) w -> p (a c) (r w)", r=2)
                             ).then_inc(x_loaded.sem, 16)

            def load_halo(b):
                if isinstance(b, int) and b == 0:
                    sp.wait_ge(picture0_step, 3)
                else:
                    sp.wait_ge(product_added.sem, product_added.at(b - 1, 1))
                sp.dma_start(gray[1:P, 0, 1:D + 1], gray[0:P - 1, 2, 1:D + 1]).then_inc(halo_in.sem, 16)
                sp.dma_start(gray[0:P - 1, 3, 1:D + 1], gray[1:P, 1, 1:D + 1]).then_inc(halo_in.sem, 16)

            def write_parts(b, tiles):
                if tiles[0] == 0 and not (isinstance(b, int) and b == 0):
                    for g in range(NG):
                        sp.wait_ge(stack_in[g].sem, stack_in[g].at(b - 1))
                for m in tiles:
                    sp.wait_ge(parts_made.sem, parts_made.at(b, PLACE["qk", m]))
                    sp.dma_start(parts_dram[:, m].rearrange("a p t -> p a t"), parts[:, :, m, :]
                                 ).then_inc(parts_out.sem, 16)

            def load_stack(b, g):
                sp.wait_ge(parts_out.sem, parts_out.at(b, 1 if g == 0 else None))
                sp.sem_inc(sp_passed, 1)
                if not (isinstance(b, int) and b == 0):
                    sp.wait_ge(st_made.sem, st_made.at(b - 1, 12 * g + 11))
                m, row = head_rows(g)
                for i, (pq, pk) in enumerate(PARTS):
                    for dst, part, tile in ((q_st, pq, m), (k_st, pk, 2 + m)):
                        sp.dma_start(dst[DH * i:DH * i + DH, G * g:G * g + G, :],
                                     parts_dram[part, tile, row:row + G * DH, :]
                                     .rearrange("(h d) t -> d h t", d=DH)).then_inc(stack_in[g].sem, 16)

            def send_shift(b, g):
                sp.wait_ge(taken["shift"].sem, taken["shift"].at(b, g))
                sp.dma_start(shift_dram[:, G * g:G * g + G, :], shift_T[:, :]).then_inc(shift_out.sem, 16)

            def bring_shift(b, g):
                sp.wait_ge(shift_out.sem, shift_out.at(b, g))
                for a in range(3):
                    sp.dma_start(q_st[KROWS + a:KROWS + a + 1, G * g:G * g + G, :],
                                 shift_dram[a:a + 1, G * g:G * g + G, :]).then_inc(shift_in[g].sem, 16)

            def store_rows(dram, picture, text, b, done):
                pic = dram[bass.ds(b, 1), 0:IMG, :].rearrange("a (p r) d -> p (a r) d", r=2)
                sp.dma_start(pic, picture).then_inc(done.sem, 16)
                txt = dram[bass.ds(b, 1), IMG:TOK, :].rearrange("a p d -> p (a d)")
                sp.dma_start(txt, text).then_inc(done.sem, 16)

            def store_gated(b):
                sp.wait_ge(gated_made.sem, gated_made.at(b))
                store_rows(gated_dram, xn2[:, 0:2, :], xn2[:, 2, :], b, gated_out)

            def store_out(b):
                sp.wait_ge(taken["down"].sem, taken["down"].at(b))
                store_rows(out, h[:, bass.ds(b * NT, 2), :], h[:, bass.ds(b * NT + 2, 1), :].rearrange("p a d -> p (a d)"),
                           b, rows_out)

            def load_weight(i, dst, src):
                sp.dma_start(dst, src).then_inc(weights_in[i], 16)

            load_x(0)
            with nc.allow_non_contiguous_dma(reason="1024 token numbers"):
                sp.dma_start(ids[:, :], x_txt.rearrange("b t -> t b")).then_inc(ids_in, 16)
            sp.dma_start(lora_b, lora_B).then_inc(small_in, 16)
            sp.dma_start(taps[:, :, :].rearrange("p f k -> p (f k)"),
                         scharr.rearrange("f a u v -> (f a u v)").partition_broadcast(P)
                         ).then_inc(small_in, 16)
            load_weight(0, raw[0][:, 0:DC * 3 * D].rearrange("p (c n) -> p c n", c=DC),
                        w_qkvT.rearrange("(c p) n -> p c n", p=P))
            load_weight(1, raw[1][:, 0:DC * D].rearrange("p (c n) -> p c n", c=DC),
                        w_outT.rearrange("(c p) n -> p c n", p=P))
            load_weight(1, raw[1][:, DC * D:DC * D + DC * E].rearrange("p (c n) -> p c n", c=DC),
                        router.rearrange("(c p) n -> p c n", p=P))
            load_halo(0)
            load_x(1)
            sp.wait_ge(w_split, 1)
            load_weight(2, raw[0][:, 0:DC * F].rearrange("p (c n) -> p c n", c=DC),
                        ws1.rearrange("(c p) n -> p c n", p=P))
            sp.wait_ge(w_split, 3)
            load_weight(3, raw[1][:, 0:DC * F].rearrange("p (c n) -> p c n", c=DC),
                        ws3.rearrange("(c p) n -> p c n", p=P))
            load_halo(1)
            load_x(2)
            write_parts(0, (0, 2))
            load_stack(0, 0)
            write_parts(0, (1, 3))
            sp.wait_ge(w_split, 4)
            load_weight(4, raw[0][:, 0:(NF - 1) * D].rearrange("p (c n) -> p c n", c=NF - 1),
                        ws2[0:(NF - 1) * P, :].rearrange("(c p) n -> p c n", p=P))
            load_weight(4, raw[0][0:FT[-1], (NF - 1) * D:NF * D], ws2[(NF - 1) * P:F, :])
            load_stack(0, 1)
            send_shift(0, 0)
            load_stack(0, 2)
            bring_shift(0, 0)
            load_stack(0, 3)

            def body(j, front, back, conv, load, carry):
                f, b = j + 1, j - 1
                if carry:
                    load_stack(j, 3)
                send_shift(j, 1)
                bring_shift(j, 1)
                if conv:
                    load_halo(j + 2)
                if load:
                    load_x(j + 3)
                if front:
                    write_parts(f, (0, 2))
                    load_stack(f, 0)
                send_shift(j, 2)
                bring_shift(j, 2)
                if front:
                    write_parts(f, (1, 3))
                send_shift(j, 3)
                if front:
                    load_stack(f, 1)
                bring_shift(j, 3)
                if back:
                    store_gated(b)
                if front:
                    send_shift(f, 0)
                    load_stack(f, 2)
                    bring_shift(f, 0)
                if back:
                    store_out(b)

            body(0, True, False, True, True, False)
            with sp.Fori(1, NB - 3) as j:
                body(j, True, True, True, True, True)
            body(NB - 3, True, True, True, False, True)
            body(NB - 2, True, True, False, False, True)
            body(NB - 1, False, True, False, False, True)

            def load_expert(e):
                sl = e % 3
                sp.dma_start(wx[0][:, sl], w1[e].rearrange("(c p) n -> p c n", p=P)).then_inc(expert_in[e % 2], 16)
                sp.dma_start(wx[1][:, sl], w3[e].rearrange("(c p) n -> p c n", p=P)).then_inc(expert_in[e % 2], 16)
                sp.dma_start(wx[2][:, sl, 0:NF - 1], w2[e, 0:(NF - 1) * P, :].rearrange("(c p) n -> p c n", p=P)
                             ).then_inc(expert_in[e % 2], 16)
                sp.dma_start(wx[2][0:FT[-1], sl, NF - 1], w2[e, (NF - 1) * P:F, :]).then_inc(expert_in[e % 2], 16)

            sp.wait_ge(pv_made.sem, pv_made.at(NB - 1))
            for e in range(3):
                load_expert(e)
                if e:
                    sp.wait_ge(expert_in[(e - 1) % 2], 64 * ((e - 1) // 2 + 1))
                    sp.sem_inc(expert_ready, 1)
                if e == 1:
                    store_gated(NB - 1)
            store_out(NB - 1)
            sp.wait_ge(routed, 1)
            for e in range(3, E):
                first = sp.value_load(route_i[0:1, 2 * TILES + e - 2:2 * TILES + e - 1], min_val=0, max_val=TILES)
                sp.wait_ge(e_down, first)
                load_expert(e)
                sp.wait_ge(expert_in[(e - 1) % 2], 64 * ((e - 1) // 2 + 1))
                sp.sem_inc(expert_ready, 1)
            sp.wait_ge(expert_in[(E - 1) % 2], 64 * ((E - 1) // 2 + 1))
            sp.sem_inc(expert_ready, 1)

        @block.gpsimd
        def _(pool):
            made_n = [0]

            def const(ins):
                made_n[0] += 1
                ins.then_inc(consts_made, 1)

            const(nc.gpsimd.memset(gray[:, :, :], 0.0))
            const(nc.gpsimd.memset(ident[:, :], 0.0))
            const(nc.gpsimd.memset(identb[:, :], 0.0))
            const(nc.gpsimd.memset(onesb[:, :], 1.0))
            const(nc.gpsimd.memset(minus_half[:, :], -0.5))
            pool.wait_ge(consts_made, made_n[0])
            const(nc.gpsimd.affine_select(out=ident[:, :], in_=ident[:, :], compare_op=ALU.not_equal, fill=1.0,
                                          base=0, pattern=[[-1, P]], channel_multiplier=1))
            const(nc.gpsimd.affine_select(out=identb[:, :], in_=identb[:, :], compare_op=ALU.not_equal, fill=1.0,
                                          base=0, pattern=[[-1, P]], channel_multiplier=1))
            const(nc.gpsimd.affine_select(out=before[:, :], in_=onesb[:, :], compare_op=ALU.is_gt, fill=0.0,
                                          base=0, pattern=[[1, P]], channel_multiplier=-1))
            assert made_n[0] == FIRST_CONSTS

            def add_product(b, n):
                pool.wait_ge(product_made.sem, product_made.at(b - 1, n))
                if not (isinstance(b, int) and b == 1 and n == 0):
                    pool.wait_ge(product_added.sem, product_added.at(b - 1, n - 1))
                into = gray[:, 1:3, 1:D + 1] if n < 2 else edge[:, (n - 2) // 8]
                nc.gpsimd.tensor_tensor(into, into, product[:, n % 2], ALU.add).then_inc(product_added.sem, 1)

            def norm_scale(which, b):
                pool.wait_ge(ln_aggr[which].sem, ln_aggr[which].at(b))
                pool.sem_inc(pool_passed, 1)
                nc.gpsimd.tensor_scalar(rstd[:, which, :], mv[:, which, :, 1], EPS, None, ALU.add
                                        ).then_inc(ln_rstd[which].sem, 1)
                pool.wait_ge(ln_rstd[which].sem, ln_rstd[which].at(b, 0))
                nc.gpsimd.tensor_tensor(rstd[:, which, :], rstd[:, which, :], minus_half[:, :], ALU.pow
                                        ).then_inc(ln_rstd[which].sem, 1)

            def low_mid(b, f):
                n = FT[f]
                pool.wait_ge(mid_high.sem, mid_high.at(b, f))
                nc.gpsimd.tensor_tensor(mid[1][0:n, f, :], mid_f[0:n, f % 2, :], mid[0][0:n, f, :].bitcast(F32),
                                        ALU.subtract).then_inc(mid_low.sem, 1)

            def part3(b, m):
                n = PLACE["qk", m]
                pool.wait_ge(part2_made.sem, part2_made.at(b, n))
                nc.gpsimd.tensor_tensor(parts[:, 2, m, :], rest[:, n % 2, :], parts[:, 1, m, :], ALU.subtract
                                        ).then_inc(parts_made.sem, 1)

            pool.wait_ge(ids_step, 3)
            for b in range(NB):
                nc.gpsimd.indirect_dma_start(lora_a[:, b, :], None, lora_A[:, :],
                                             bass.IndirectOffsetOnAxis(ids[:, b:b + 1], 0)).then_inc(lora_in, 16)
            for b in range(NB):
                nc.gpsimd.indirect_dma_start(h[:, NT * b + 2, :], None, base_rows[:, :],
                                             bass.IndirectOffsetOnAxis(ids[:, b:b + 1], 0)).then_inc(text_in, 16)
            const(nc.gpsimd.memset(v_sb, 1.0))
            pool.wait_ge(consts_made, made_n[0])
            const(nc.gpsimd.memset(k_st[KROWS:KROWS + 3], 1.0))
            pool.wait_ge(consts_made, made_n[0])
            assert made_n[0] == CORE_CONSTS
            norm_scale(0, 0)
            for n in range(2):
                add_product(1, n)
            for m in (0, 2, 1, 3):
                part3(0, m)
            for n in range(2, 18):
                add_product(1, n)
            const(nc.gpsimd.iota(iota_p[:, :], [[1, P]], base=0, channel_multiplier=0, allow_small_or_imprecise_dtypes=True))
            const(nc.gpsimd.iota(iota_t[:, :], [[1, TILES]], base=0, channel_multiplier=0, allow_small_or_imprecise_dtypes=True))
            const(nc.gpsimd.iota(iota_e[:, :], [[1, E]], base=-E, channel_multiplier=0, allow_small_or_imprecise_dtypes=True))
            const(nc.gpsimd.iota(iota_k[:, :], [[P, COLS]], base=0, channel_multiplier=0, allow_small_or_imprecise_dtypes=True))
            const(nc.gpsimd.memset(lower_e[:, :, :], 1.0))
            pool.wait_ge(consts_made, made_n[0])
            const(nc.gpsimd.affine_select(out=lower_e[:, :, :], in_=lower_e[:, :, :], compare_op=ALU.is_gt, fill=0.0,
                                          base=0, pattern=[[1, E], [-1, E]], channel_multiplier=0))
            const(nc.gpsimd.iota(token[:, :, 0:2], [[TOK, NB], [1, 2]], base=-NTOK, channel_multiplier=2))
            const(nc.gpsimd.iota(token[:, :, 2:3], [[TOK, NB]], base=IMG - NTOK, channel_multiplier=1))
            assert made_n[0] == CONSTS
            norm_scale(0, 1)

            def body(j, front, back, conv):
                b, c = j - 1, j + 2
                for q in range(HALVES):
                    if q == 6 and back:
                        norm_scale(1, b)
                    for at_q, what, n, _ in USES:
                        if at_q == q - 1 and what == "qk" and front:
                            part3(j + 1, n)
                    if q in SPLIT_AT and back:
                        low_mid(b, SPLIT_AT[q])
                    for n in range(18):
                        if PRODUCT_AT[n] == q and conv:
                            add_product(c, n)
                    if q == 21 and conv:
                        norm_scale(0, c)

            body(0, True, False, True)
            with pool.Fori(1, NB - 2) as j:
                body(j, True, True, True)
            body(NB - 2, True, True, False)
            body(NB - 1, False, True, False)
            norm_scale(1, NB - 1)
            for f in range(NF):
                low_mid(NB - 1, f)

            def gather(k, i):
                nc.gpsimd.indirect_dma_start(xg[:, i, :], None, gated_rows,
                                             bass.IndirectOffsetOnAxis(slot_i[:, i:i + 1], 0),
                                             bounds_check=NTOK - 1, oob_is_err=False).then_inc(row_in[i], 16)

            def pick_slots(k, i, n):
                nc.gpsimd.tensor_copy(slot_i[:, i:i + 1], slot_of[:, bass.ds(k, 1)]).then_inc(slot_picked, 1)
                pool.wait_ge(slot_picked, n)
                pool.sem_inc(pool_passed, 1)

            def scatter(k, i, n):
                if not (isinstance(k, int) and k < 2):
                    pool.wait_ge(row_out[i], (k - i) * 8)
                pick_slots(k, 2 + i, n)
                pool.wait_ge(e_y, k + 1)
                pool.sem_inc(pool_passed, 1)
                nc.gpsimd.indirect_dma_start(out_rows, bass.IndirectOffsetOnAxis(slot_i[:, 2 + i:3 + i], 0), y_e[:, i, :],
                                             None, bounds_check=NTOK - 1, oob_is_err=False, compute_op=ALU.add
                                             ).then_inc(row_out[i], 16)

            nc.gpsimd.memset(xg, 0.0).then_inc(row_cleared, 1)
            pool.wait_ge(row_cleared, 1)
            pool.wait_ge(routed, 1)
            pool.wait_ge(gated_out.sem, gated_out.at(NB - 1))
            for i in range(2):
                pick_slots(i, i, i + 1)
                gather(i, i)

            def turn(k, i, last):
                if not last:
                    pool.wait_ge(e_xT, k + 2)
                    pick_slots(k + 3, 1 - i, 2 * k + 4)
                    gather(k + 3, 1 - i)
                    scatter(k, i, 2 * k + 5)
                else:
                    scatter(k, i, TILES + k + 1)

            pool.wait_ge(e_xT, 1)
            pick_slots(2, 0, 3)
            gather(2, 0)
            pool.wait_ge(rows_out.sem, rows_out.at(NB - 1))
            turn(0, 0, False)
            turn(1, 1, False)
            with pool.Fori(2, TILES - 4, 2) as k:
                turn(k, 0, False)
                turn(k + 1, 1, False)
            turn(TILES - 3, 0, True)
            turn(TILES - 2, 1, True)
            turn(TILES - 1, 0, True)
            pool.wait_ge(row_out[0], 16 * (TILES // 2 + 1))
            pool.wait_ge(row_out[1], 16 * (TILES // 2))

        @block.scalar
        def _(act):
            def begin_gray(b):
                act.wait_ge(x_loaded.sem, x_loaded.at(b))
                if isinstance(b, int) and b == 1:
                    act.wait_ge(picture0_step, PICTURE0)
                nc.scalar.activation(gray[:, 1:3, 1:D + 1], x_in[:, 0], ACT.Copy, scale=GRAY[0]
                                     ).then_inc(gray_begun.sem, 1)

            def make_product(b, n):
                if not (isinstance(b, int) and b == 1 and n < 2):
                    act.wait_ge(product_added.sem, product_added.at(b - 1, n - 2))
                if n < 2:
                    act.wait_ge(gray_begun.sem, gray_begun.at(b - 1))
                    nc.scalar.activation(product[:, n % 2], x_in[:, n + 1], ACT.Copy, scale=GRAY[n + 1]
                                         ).then_inc(product_made.sem, 1)
                else:
                    f, k = divmod(n - 2, 8)
                    nc.scalar.activation(product[:, n % 2], gray_rows(k + 1), ACT.Copy, scale=taps[:, f, k + 1:k + 2]
                                         ).then_inc(product_made.sem, 1)

            def first_taps(b):
                act.wait_ge(halo_in.sem, halo_in.at(b))
                act.wait_ge(edge_step.sem, edge_step.at(b - 1))
                for f in range(2):
                    nc.scalar.activation(edge[:, f], gray_rows(0), ACT.Copy, scale=taps[:, f, 0:1]
                                         ).then_inc(first_tap.sem, 1)
                act.wait_ge(first_tap.sem, first_tap.at(b - 1))

            def exps(j, step, half):
                for hh in (2 * half, 2 * half + 1):
                    act.wait_ge(st_made.sem, st_made.at(j, 4 * step + hh))
                    if not (isinstance(j, int) and j == 0 and step < 3):
                        act.wait_ge(pv_made.sem, pv_made.at(j, step - 3))
                    nc.scalar.activation(probs[:, step % 3, hh, :], st_ps[:, hh % 2, 0:TOK], ACT.Exp,
                                         scale=DH ** -0.5).then_inc(exp_made.sem, 1)

            def copy_high(kind, n, b, dst):
                act.wait_ge(made[kind].sem, made[kind].at(b, n))
                nc.scalar.activation(dst[0][:, n, :], bank(kind, n)[:, 0:TOK], ACT.Copy).then_inc(high[kind].sem, 1)

            def copy_ot(j, g):
                act.wait_ge(pv_made.sem, pv_made.at(j, 3 * g + 2))
                if not (isinstance(j, int) and j == 0 and g == 0):
                    act.wait_ge(made["attn_back"].sem, made["attn_back"].at(j, g - 1))
                nc.scalar.activation(ot[:, :], pv_ps[:, 0:TOK], ACT.Copy).then_inc(ot_copied.sem, 1)

            def copy_shift(b, g):
                act.wait_ge(made["shift"].sem, made["shift"].at(b, g))
                if not (isinstance(b, int) and b == 0 and g == 0):
                    act.wait_ge(shift_out.sem, shift_out.at(b, g - 1))
                nc.scalar.activation(shift_T[:, :], bank("shift", g).bitcast(BF16)[0:3 * G, 0:TOK], ACT.Copy
                                     ).then_inc(taken["shift"].sem, 1)

            def part1(b, m):
                n = PLACE["qk", m]
                act.wait_ge(made["qk"].sem, made["qk"].at(b, n))
                if not (isinstance(b, int) and b == 0):
                    act.wait_ge(parts_out.sem, parts_out.at(b - 1))
                nc.scalar.activation(parts[:, 0, m, :], bank("qk", m)[:, 0:TOK], ACT.Copy).then_inc(high["qk"].sem, 1)

            def part2(b, m):
                n = PLACE["qk", m]
                act.wait_ge(taken["qk"].sem, taken["qk"].at(b, n))
                nc.scalar.activation(parts[:, 1, m, :], rest[:, n % 2, :], ACT.Copy).then_inc(part2_made.sem, 1)

            def copy_v(b, t):
                act.wait_ge(made["v"].sem, made["v"].at(b, t))
                if not (isinstance(b, int) and b == 0):
                    act.wait_ge(pv_made.sem, pv_made.at(b - 1))
                nc.scalar.activation(v_sb[:, t, :, 0:DH], bank("v", t)[:, 0:D].rearrange("p (h d) -> p h d", h=HEADS),
                                     ACT.Copy).then_inc(taken["v"].sem, 1)

            def tanh_of(b, f):
                act.wait_ge(made["gate"].sem, made["gate"].at(b, f))
                act.wait_ge(taken["gate"].sem, taken["gate"].at(b, f - 2) if f >= 2 else taken["gate"].at(b - 1))
                n = FT[f]
                nc.scalar.activation(tanh[0:n, f % 2, :], bank("gate", f)[0:n, 0:TOK], ACT.Tanh, scale=0.5
                                     ).then_inc(tanh_made.sem, 1)

            def high_mid(b, f):
                act.wait_ge(taken["up"].sem, taken["up"].at(b, f))
                if not (isinstance(b, int) and b == 0):
                    act.wait_ge(made["down"].sem, made["down"].at(b - 1))
                n = FT[f]
                nc.scalar.activation(mid[0][0:n, f, :], mid_f[0:n, f % 2, :], ACT.Copy).then_inc(mid_high.sem, 1)

            def gate_exponential(b):
                act.wait_ge(best_found.sem, best_found.at(b))
                if not (isinstance(b, int) and b == 0):
                    act.wait_ge(gated_made.sem, gated_made.at(b - 1))
                nc.scalar.activation(gate[:, :], best[:, :], ACT.Exp, scale=-1.0).then_inc(gate_exp.sem, 1)

            act.wait_ge(taps_halved, 1)
            for n in range(2):
                act.wait_ge(made["loraT"].sem, n + 1)
                nc.scalar.activation(lora_aT[:, 4 * P * n:4 * P * n + 4 * P], bank("loraT", n)[0:RANK, :], ACT.Copy
                                     ).then_inc(taken["loraT"].sem, 1)
            begin_gray(1)
            for n in range(2):
                make_product(1, n)
            for n in range(2):
                copy_high("xT", n, 0, xT)
            for m in (0, 2, 1, 3):
                part1(0, m)
                part2(0, m)
            first_taps(1)
            for n in range(2, 18):
                make_product(1, n)
                if n == 13:
                    copy_shift(0, 0)
            act.wait_ge(consts_made, CORE_CONSTS)
            for t in range(NT):
                copy_v(0, t)
            act.wait_ge(w_split, SPLITS)

            def body(j, front, back, conv, end=False):
                f, b, c = j + 1, j - 1, j + 2
                for q in range(HALVES):
                    if not end:
                        exps(j, q // 2, q % 2)
                    if q in (6, 12, 18) and not end:
                        copy_ot(j, q // 6 - 1)
                    for at_q, what, n, _ in USES:
                        if at_q == q - 1 and what == "qk" and front:
                            part2(f, n)
                    for at_q, what, n, ahead in USES:
                        if at_q != q or not {1: front, 0: not end, -1: back}[ahead]:
                            continue
                        if what == "shift":
                            copy_shift(j + ahead, n)
                        elif what == "xT":
                            copy_high("xT", n, f, xT)
                        elif what == "attnT":
                            if n == 0 and not (isinstance(b, int) and b == 0):
                                act.wait_ge(made["up"].sem, made["up"].at(b - 1))
                            copy_high("attnT", n, b, attnT)
                        elif what == "x2T":
                            if n == 0:
                                act.wait_ge(made["proj"].sem, made["proj"].at(b))
                            copy_high("x2T", n, b, x2T)
                        elif what == "qk":
                            part1(f, n)
                        elif what == "router":
                            act.wait_ge(router_made.sem, router_made.at(b))
                            if not (isinstance(b, int) and b == 0):
                                act.wait_ge(taken["up"].sem, taken["up"].at(b - 1))
                            nc.scalar.activation(router_T, bank("router", 0)[0:E, 0:TOK], ACT.Copy
                                                 ).then_inc(router_copied.sem, 1)
                        elif what == "gate":
                            tanh_of(b, n)
                            if n == 0:
                                gate_exponential(b)
                    if q in SPLIT_AT and back:
                        high_mid(b, SPLIT_AT[q])
                    if q == 0 and conv:
                        begin_gray(c)
                    if q == 5 and conv:
                        first_taps(c)
                    for n in range(18):
                        if PRODUCT_AT[n] == q and conv:
                            make_product(c, n)
                if not end:
                    copy_ot(j, 3)
                if front:
                    for t in range(NT):
                        copy_v(f, t)

            body(0, True, False, True)
            with act.Fori(1, NB - 2) as j:
                body(j, True, True, True)
            body(NB - 2, True, True, False)
            body(NB - 1, False, True, False)
            body(NB, False, True, False, end=True)

            def e_transposed(k):
                act.wait_ge(e_xT, k + 1)
                if not (isinstance(k, int) and k == 0):
                    act.wait_ge(e_up, k)
                nc.scalar.activation(xT_e, pv_ps[:, 0:D], ACT.Copy).then_inc(e_xT_copied, 1)

            def e_gate(k):
                act.wait_ge(e_gate_made, k + 1)
                if not (isinstance(k, int) and k == 0):
                    act.wait_ge(e_u, k)
                nc.scalar.activation(tanh_e, st_ps[:, :, 0:HF], ACT.Tanh, scale=0.5).then_inc(e_tanh, 1)

            def e_mid_transposed(k):
                act.wait_ge(e_midT, k + 1)
                if not (isinstance(k, int) and k == 0):
                    act.wait_ge(e_down, k)
                nc.scalar.activation(midT_e[:, 0:4 * P], work[:, 0, :], ACT.Copy).then_inc(e_midT_a, 1)

            def e_result(k, i):
                act.wait_ge(e_down, k + 1)
                if not (isinstance(k, int) and k < 2):
                    act.wait_ge(row_out[i], (k - i) * 8)
                nc.scalar.activation(y_e[:, i, :], work[:, 2, 0:D], ACT.Copy).then_inc(e_y, 1)

            e_transposed(0)
            e_gate(0)
            e_transposed(1)
            def two_tiles(k):
                for i in (1, 0):
                    kk = k + 1 - i
                    e_gate(kk)
                    e_mid_transposed(kk - 1)
                    e_transposed(kk + 1)
                    e_result(kk - 1, 1 - i)

            two_tiles(1)
            with act.Fori(3, TILES - 2, 2) as k:
                two_tiles(k)
            for kk in (TILES - 2, TILES - 1):
                e_gate(kk)
                e_mid_transposed(kk - 1)
                if kk < TILES - 1:
                    e_transposed(kk + 1)
                e_result(kk - 1, (kk - 1) % 2)
            e_mid_transposed(TILES - 1)
            e_result(TILES - 1, 0)

        @block.vector
        def _(dve):
            V = nc.vector
            dve.wait_ge(ids_in, 16)
            V.tensor_scalar(ids_n[:, :], ids[:, :], 0, VOCAB, ALU.is_lt, ALU.mult).then_inc(ids_step, 1)
            dve.wait_ge(ids_step, 1)
            V.tensor_tensor(ids_n[:, :], ids_n[:, :], ids[:, :], ALU.add).then_inc(ids_step, 1)
            dve.wait_ge(ids_step, 2)
            V.tensor_scalar(ids[:, :], ids_n[:, :], VOCAB - 1, 0, ALU.min, ALU.max).then_inc(ids_step, 1)

            splits = [0]

            def split(dst, src, loaded, count):
                dve.wait_ge(weights_in[loaded], count)
                splits[0] += 1
                V.tensor_copy(dst[0], src).then_inc(w_high, 1)
                dve.wait_ge(w_high, splits[0])
                V.tensor_tensor(dst[1], src, dst[0].bitcast(F32), ALU.subtract).then_inc(w_split, 1)

            def as3(room_, c):
                return room_.rearrange("p (c n) -> p c n", c=c)

            def edges(b, filters=range(2)):
                for f in filters:
                    if isinstance(b, int) and b == 0:
                        dve.wait_ge(picture0_step, PICTURE0)
                    else:
                        dve.wait_ge(product_added.sem, product_added.at(b - 1, 9 + 8 * f))
                    V.scalar_tensor_tensor(out=edge[:, f], in0=edge[:, f], scalar=-1.0, in1=edge[:, f],
                                           op0=ALU.mult, op1=ALU.max).then_inc(edge_step.sem, 1)
                if 1 not in filters:
                    return
                dve.wait_ge(edge_step.sem, edge_step.at(b, 1))
                V.tensor_tensor(h[:, bass.ds(b * NT, 2), :], edge[:, 0], edge[:, 1], ALU.add).then_inc(edge_step.sem, 1)

            def norm_stats(which, b, tiles=range(NT)):
                if not (isinstance(b, int) and b == 0):
                    dve.wait_ge(ln_done[which].sem, ln_done[which].at(b - 1))
                dve.sem_inc(dve_passed, 1)
                for t in tiles:
                    V.bn_stats(stats[:, which, t, :], h[:, bass.ds(b * NT + t, 1), :].rearrange("p a d -> p (a d)")
                               ).then_inc(ln_stats[which].sem, 1)

            def norm_aggr(which, b):
                dve.wait_ge(ln_stats[which].sem, ln_stats[which].at(b))
                dve.sem_inc(dve_passed, 1)
                for t in range(NT):
                    V.bn_aggr(mv[:, which, t, :], stats[:, which, t, :]).then_inc(ln_aggr[which].sem, 1)

            def norm_apply(which, b, dst, tiles=range(NT)):
                dve.wait_ge(ln_rstd[which].sem, ln_rstd[which].at(b))
                for t in tiles:
                    V.tensor_scalar(dst[:, t, :], h[:, bass.ds(b * NT + t, 1), :].rearrange("p a d -> p (a d)"),
                                    mv[:, which, t, 0:1], rstd[:, which, t:t + 1], ALU.subtract, ALU.mult
                                    ).then_inc(ln_done[which].sem, 1)

            def low_part(kind, n, b, dst):
                dve.wait_ge(high[kind].sem, high[kind].at(b, n))
                V.tensor_tensor(dst[1][:, n, :], bank(kind, n)[:, 0:TOK], dst[0][:, n, :].bitcast(F32), ALU.subtract
                                ).then_inc(taken[kind].sem, 1)

            def rest_of(b, m):
                n = PLACE["qk", m]
                dve.wait_ge(high["qk"].sem, high["qk"].at(b, n))
                if not (isinstance(b, int) and b == 0 and n < 2):
                    dve.wait_ge(parts_made.sem, parts_made.at(b, n - 2))
                V.tensor_tensor(rest[:, n % 2, :], bank("qk", m)[:, 0:TOK], parts[:, 0, m, :], ALU.subtract
                                ).then_inc(taken["qk"].sem, 1)

            def maxima(b, g, i):
                hh, t = divmod(i, NT)
                n = 12 * g + i
                if i == 0 and not (isinstance(b, int) and b == 0 and g == 0):
                    dve.wait_ge(shift_split.sem, shift_split.at(b, g - 1))
                dve.wait_ge(smax_made.sem, smax_made.at(b, n))
                V.reduce_max(smax[:, t, hh:hh + 1], sm_ps[:, n % 2, 0:TOK], axis=AX.X).then_inc(smax_found.sem, 1)

            def split_shift(b, g):
                dve.wait_ge(smax_found.sem, smax_found.at(b, 12 * g + 11))
                if not (isinstance(b, int) and b == 0 and g == 0):
                    dve.wait_ge(made["shift"].sem, made["shift"].at(b, g - 1))
                V.tensor_scalar(shift_p[:, :, 0, :], smax[:, :, :], -1.0, None, ALU.mult).then_inc(shift_step.sem, 1)
                dve.wait_ge(shift_step.sem, shift_step.at(b, 3 * g))
                V.scalar_tensor_tensor(out=smax_r[:, :, :], in0=smax[:, :, :], scalar=-1.0, in1=shift_p[:, :, 0, :],
                                       op0=ALU.mult, op1=ALU.subtract).then_inc(shift_step.sem, 1)
                dve.wait_ge(shift_step.sem, shift_step.at(b, 3 * g + 1))
                V.tensor_copy(shift_p[:, :, 1, :], smax_r[:, :, :]).then_inc(shift_step.sem, 1)
                dve.wait_ge(shift_step.sem, shift_step.at(b, 3 * g + 2))
                V.tensor_tensor(shift_p[:, :, 2, :], smax_r[:, :, :], shift_p[:, :, 1, :], ALU.subtract
                                ).then_inc(shift_split.sem, 1)

            def normalise(j, g):
                dve.wait_ge(made["attn_back"].sem, made["attn_back"].at(j, g))
                if not (isinstance(j, int) and j == 0 and g == 0):
                    dve.wait_ge(taken["attn_back"].sem, taken["attn_back"].at(j, g - 1))
                rows = bank("attn_back", g)[:, 0:NT * P].rearrange("p (t h d) -> p t h d", t=NT, h=G)
                V.reciprocal(rden[:, :, :], rows[:, :, :, DH]).then_inc(rden_made.sem, 1)
                dve.wait_ge(rden_made.sem, rden_made.at(j, g))
                V.tensor_tensor(attn[:, :, G * DH * g:G * DH * (g + 1)].rearrange("p t (h d) -> p t h d", h=G),
                                rows[:, :, :, 0:DH], rden[:, :, :].unsqueeze(3).to_broadcast([P, NT, G, DH]), ALU.mult
                                ).then_inc(taken["attn_back"].sem, 1)

            def add_to_rows(kind, b, t):
                dve.wait_ge(made[kind].sem, made[kind].at(b, t))
                row = h[:, bass.ds(b * NT + t, 1), :].rearrange("p a d -> p (a d)")
                V.tensor_tensor(row, bank(kind, t)[:, 0:D], row, ALU.add).then_inc(taken[kind].sem, 1)

            def take_scores(b):
                dve.wait_ge(made["router"].sem, made["router"].at(b))
                V.tensor_copy(scores8[:, bass.ds(b * NT, NT), :],
                              bank("router", 0)[:, TOK:TOK + NT * E].rearrange("p (t e) -> p t e", t=NT)
                              ).then_inc(taken["router"].sem, 1)
                dve.wait_ge(taken["router"].sem, taken["router"].at(b))
                dve.sem_inc(dve_passed, 1)
                V.reduce_max(best[:, :], scores8[:, bass.ds(b * NT, NT), :], axis=AX.X).then_inc(best_found.sem, 1)

            def gate_rows(b):
                dve.wait_ge(gate_exp.sem, gate_exp.at(b))
                V.tensor_scalar(gate[:, :], gate[:, :], 1.0, None, ALU.add).then_inc(gate_step.sem, 1)
                dve.wait_ge(gate_step.sem, gate_step.at(b, 0))
                V.reciprocal(gate[:, :], gate[:, :]).then_inc(gate_step.sem, 1)
                dve.wait_ge(gate_step.sem, gate_step.at(b, 1))
                for t in range(NT):
                    V.tensor_scalar(xn2[:, t, :], xn2[:, t, :], gate[:, t:t + 1], None, ALU.mult
                                    ).then_inc(gated_made.sem, 1)

            def double_silu(b, f):
                n = FT[f]
                dve.wait_ge(tanh_made.sem, tanh_made.at(b, f))
                if not (isinstance(b, int) and b == 0 and f == 0):
                    dve.wait_ge(taken["up"].sem, taken["up"].at(b, f - 1))
                V.scalar_tensor_tensor(out=half_u[0:n, :], in0=tanh[0:n, f % 2, :], scalar=1.0,
                                       in1=bank("gate", f)[0:n, 0:TOK], op0=ALU.add, op1=ALU.mult
                                       ).then_inc(taken["gate"].sem, 1)

            def middle(b, f):
                n = FT[f]
                dve.wait_ge(taken["gate"].sem, taken["gate"].at(b, f))
                dve.wait_ge(made["up"].sem, made["up"].at(b, f))
                dve.wait_ge(mid_low.sem, mid_low.at(b, f - 2) if f >= 2 else mid_low.at(b - 1))
                V.scalar_tensor_tensor(out=mid_f[0:n, f % 2, :], in0=half_u[0:n, :], scalar=0.5,
                                       in1=bank("up", f)[0:n, 0:TOK], op0=ALU.mult, op1=ALU.mult
                                       ).then_inc(taken["up"].sem, 1)

            pic_n = [0]

            def pic_step(ins):
                pic_n[0] += 1
                ins.then_inc(picture0_step, 1)
                dve.wait_ge(picture0_step, pic_n[0])

            dve.wait_ge(small_in, 32)
            V.tensor_scalar(taps[:, :, :], taps[:, :, :], 0.5, None, ALU.mult).then_inc(taps_halved, 1)
            dve.wait_ge(taps_halved, 1)
            dve.wait_ge(consts_made, FIRST_CONSTS)
            dve.wait_ge(x_loaded.sem, x_loaded.at(0))
            middle_rows = gray[:, 1:3, 1:D + 1]
            pic_step(V.tensor_scalar(middle_rows, x_in[:, 0], GRAY[0], None, ALU.mult))
            for i in (1, 2):
                pic_step(V.scalar_tensor_tensor(out=middle_rows, in0=x_in[:, i], scalar=GRAY[i], in1=middle_rows,
                                                op0=ALU.mult, op1=ALU.add))
            split([w[:, :, :] for w in wqkv], as3(raw[0][:, 0:DC * 3 * D], DC), 0, 16)
            for n in range(2):
                for k in range(9):
                    if n == 0 and k == 0:
                        dve.wait_ge(halo_in.sem, halo_in.at(0))
                    if k == 0:
                        pic_step(V.tensor_scalar(edge[:, n], gray_rows(0), taps[:, n, 0:1], None, ALU.mult))
                    else:
                        pic_step(V.scalar_tensor_tensor(out=edge[:, n], in0=gray_rows(k), scalar=taps[:, n, k:k + 1],
                                                        in1=edge[:, n], op0=ALU.mult, op1=ALU.add))
            assert pic_n[0] == PICTURE0
            edges(0)
            split([w[:, :, :] for w in wo], as3(raw[1][:, 0:DC * D], DC), 1, 32)
            split([w[:, :, :] for w in wr], as3(raw[1][:, DC * D:DC * D + DC * E], DC), 1, 32)
            dve.wait_ge(text_in, 16 * NB)

            def add_lora(n):
                dve.wait_ge(made["lora"].sem, n + 1)
                rows = h[:, 2 * NT * n + 2:2 * NT * n + 6:3, :]
                V.tensor_tensor(rows, bank("lora", n).rearrange("p (b d) -> p b d", b=2), rows, ALU.add
                                ).then_inc(taken["lora"].sem, 1)

            add_lora(0)
            dve.wait_ge(edge_step.sem, edge_step.at(0))
            dve.wait_ge(taken["lora"].sem, 1)
            norm_stats(0, 0)
            norm_aggr(0, 0)
            for n in range(1, 4):
                add_lora(n)
            norm_apply(0, 0, xn)
            for n in range(2):
                low_part("xT", n, 0, xT)
            for m in (0, 2, 1, 3):
                rest_of(0, m)
            split([w[:, :, :] for w in wg], as3(raw[0][:, 0:DC * F], DC), 2, 16)
            split([w[:, :, :] for w in wu], as3(raw[1][:, 0:DC * F], DC), 3, 16)
            for g in range(2):
                for i in range(12):
                    maxima(0, g, i)
                split_shift(0, g)
                if g == 0:
                    split([w[:, 0:NF - 1, :] for w in wd], as3(raw[0][:, 0:(NF - 1) * D], NF - 1), 4, 32)
                    split([w[0:FT[-1], NF - 1, :] for w in wd], raw[0][0:FT[-1], (NF - 1) * D:NF * D], 4, 32)
            assert splits[0] == SPLITS
            edges(1)
            dve.wait_ge(edge_step.sem, edge_step.at(1))
            norm_stats(0, 1)
            norm_aggr(0, 1)
            norm_apply(0, 1, xn)

            n_route = [0]

            def step(ins):
                n_route[0] += 1
                ins.then_inc(route_step, 1)
                dve.wait_ge(route_step, n_route[0])

            top = rt_small[:, 0:COLS]
            count, tiles, base, last = (rt_small[:, 32 + 8 * i:40 + 8 * i] for i in range(4))
            within, tile = rt_b[:, 0:COLS], rt_b[:, 32:32 + COLS]

            def choose_experts():
                dve.wait_ge(consts_made, CONSTS)
                step(V.reduce_max(top, scores8[:, :, :], axis=AX.X))
                step(V.tensor_tensor(rt_a, scores8[:, :, :], top.unsqueeze(2).to_broadcast([P, COLS, E]), ALU.is_equal))
                iota_eb = iota_e[:, :].unsqueeze(1).to_broadcast([P, COLS, E])
                step(V.tensor_tensor(rt_a, rt_a, iota_eb, ALU.mult))
                step(V.tensor_reduce(top, rt_a, axis=AX.X, op=ALU.min))
                V.tensor_tensor(onehot, iota_eb, top.unsqueeze(2).to_broadcast([P, COLS, E]), ALU.is_equal
                                ).then_inc(onehot_made, 1)

            def count_tiles():
                dve.wait_ge(rank_made, 1)
                step(V.tensor_copy(count, sm_ps[:, 1, 0:E]))
                step(V.tensor_tensor(rt_e24, count.unsqueeze(2).to_broadcast([P, E, COLS]),
                                     iota_k[:, :].unsqueeze(1).to_broadcast([P, E, COLS]), ALU.is_gt))
                step(V.tensor_reduce(tiles, rt_e24, axis=AX.X, op=ALU.add))
                step(V.tensor_tensor(rt_ee, lower_e[:, :, :], tiles.unsqueeze(1).to_broadcast([P, E, E]), ALU.mult))
                step(V.tensor_reduce(base, rt_ee, axis=AX.X, op=ALU.add))
                step(V.tensor_tensor(last, base, tiles, ALU.add))

            def serve_tiles():
                step(V.tensor_tensor(rt_te, iota_t[:, :].unsqueeze(2).to_broadcast([P, TILES, E]),
                                     last.unsqueeze(1).to_broadcast([P, TILES, E]), ALU.is_ge))
                expert, three, place = (rt_b[:, 32 * i:32 * i + TILES] for i in range(3))
                step(V.tensor_reduce(expert, rt_te, axis=AX.X, op=ALU.add))
                step(V.tensor_scalar(expert, expert, float(E - 1), None, ALU.min))
                step(V.tensor_scalar(three, expert, 3.0, -3.0, ALU.is_ge, ALU.mult))
                step(V.tensor_tensor(place, expert, three, ALU.add))
                step(V.tensor_scalar(three, expert, 6.0, -3.0, ALU.is_ge, ALU.mult))
                step(V.tensor_tensor(place, place, three, ALU.add))
                step(V.tensor_copy(route_i[0:1, 0:TILES], expert[0:1, :]))
                step(V.tensor_copy(route_i[0:1, TILES:2 * TILES], place[0:1, :]))
                step(V.tensor_scalar(route_i[0:1, 2 * TILES:2 * TILES + E], base[0:1, :], 1.0, None, ALU.max))

            def find_slots():
                step(V.scalar_tensor_tensor(out=rt_a, in0=base.unsqueeze(1).to_broadcast([P, COLS, E]), scalar=float(P),
                                            in1=sm_ps[:, 0, 0:COLS * E].rearrange("p (c e) -> p c e", c=COLS),
                                            op0=ALU.mult, op1=ALU.add))
                step(V.tensor_tensor(rt_a, rt_a, onehot, ALU.mult))
                step(V.tensor_reduce(top, rt_a, axis=AX.X, op=ALU.add))
                step(V.tensor_copy(rt_i[:, 0:COLS], top))
                step(V.tensor_scalar(rt_i[:, 32:32 + COLS], rt_i[:, 0:COLS], 7, None, ALU.arith_shift_right))
                step(V.tensor_scalar(rt_i[:, 0:COLS], rt_i[:, 0:COLS], P - 1, None, ALU.bitwise_and))
                step(V.tensor_copy(within, rt_i[:, 0:COLS]))
                step(V.tensor_copy(tile, rt_i[:, 32:32 + COLS]))

            def tokens_by_tile():
                tok = token[:, :, :].rearrange("p b t -> p (b t)")
                step(V.tensor_scalar(rt_i[:, 0:COLS], tok, 6, None, ALU.arith_shift_right))
                step(V.tensor_scalar(rt_i[:, 32:32 + COLS], tok, 63, None, ALU.bitwise_and))
                step(V.tensor_copy(rt_b[:, 64:64 + COLS], rt_i[:, 0:COLS]))
                step(V.tensor_copy(rt_b[:, 96:96 + COLS], rt_i[:, 32:32 + COLS]))
                step(V.tensor_tensor(tile_hot, iota_t[:, :].unsqueeze(1).to_broadcast([P, COLS, TILES]),
                                     tile.unsqueeze(2).to_broadcast([P, COLS, TILES]), ALU.is_equal))
                for i in range(2):
                    V.tensor_tensor(tile_val[:, :, i, :], tile_hot,
                                    rt_b[:, 64 + 32 * i:64 + 32 * i + COLS].unsqueeze(2).to_broadcast([P, COLS, TILES]),
                                    ALU.mult).then_inc(slot_cols, 1)

            def slot_columns(first, end):
                for c in range(first, end):
                    if c >= 12:
                        dve.wait_ge(slots_read, c - 11)
                    V.tensor_scalar(slot_hot[:, c % 12, :], iota_p[:, :], within[:, c:c + 1], None, ALU.is_equal
                                    ).then_inc(slot_cols, 1)

            def finish_slots():
                dve.wait_ge(slots_read, COLS)
                step(V.tensor_copy(rt_b[:, 0:TILES], st_ps[:, 0, TILES:2 * TILES]))
                step(V.scalar_tensor_tensor(out=rt_b[:, 32:32 + TILES], in0=st_ps[:, 0, 0:TILES], scalar=64.0,
                                            in1=rt_b[:, 0:TILES], op0=ALU.mult, op1=ALU.add))
                V.tensor_scalar(slot_of[:, :], rt_b[:, 32:32 + TILES], float(NTOK), None, ALU.add).then_inc(routed, 1)

            def body(j, front, back, conv, end=False):
                f, b, c = j + 1, j - 1, j + 2
                for q in range(HALVES):
                    g, i = [(j, 2), (j, 3), (f, 0), (f, 1)][q // 6], 2 * (q % 6)
                    if not end and (q < 12 or front):
                        maxima(g[0], g[1], i)
                        maxima(g[0], g[1], i + 1)
                        if i == 10:
                            split_shift(*g)
                    if q == 7 and back:
                        if not (isinstance(b, int) and b == 0):
                            dve.wait_ge(gated_out.sem, gated_out.at(b - 1))
                        norm_apply(1, b, xn2)
                    if q == 10 and back:
                        take_scores(b)
                    for at_q, what, n, ahead in USES:
                        if at_q != q or not {1: front, 0: not end, -1: back}[ahead]:
                            continue
                        if what == "attn_back":
                            normalise(j + ahead, n)
                        elif what == "xT":
                            low_part("xT", n, f, xT)
                        elif what == "attnT":
                            low_part("attnT", n, b, attnT)
                        elif what == "qk":
                            rest_of(f, n)
                        elif what == "proj":
                            add_to_rows("proj", b, n)
                            dve.wait_ge(taken["proj"].sem, taken["proj"].at(b, n))
                            norm_stats(1, b, [n])
                            if n == NT - 1:
                                norm_aggr(1, b)
                        elif what == "x2T":
                            low_part("x2T", n, b, x2T)
                        elif what == "gate":
                            double_silu(b, n)
                            if n == 1:
                                gate_rows(b)
                        elif what == "up":
                            middle(b, n)
                        elif what == "down":
                            add_to_rows("down", b, n)
                    if end and q == 11:
                        choose_experts()
                    if end and q == 14:
                        count_tiles()
                    if end and q == 15:
                        serve_tiles()
                    if end and q == 17:
                        find_slots()
                    if end and q == 18:
                        tokens_by_tile()
                    if end and q == 20:
                        slot_columns(0, COLS // 2)
                    if q == 13 and conv:
                        edges(c, [0])
                    if q == 18 and conv:
                        norm_stats(0, c, [2])
                    if q == 20 and conv:
                        edges(c, [1])
                    if q == 21 and conv:
                        dve.wait_ge(edge_step.sem, edge_step.at(c))
                        norm_stats(0, c, [0, 1])
                        norm_aggr(0, c)
                    if q == 22 and conv:
                        norm_apply(0, c, xn, [0])
                    if q == 23 and conv:
                        norm_apply(0, c, xn, [1, 2])

            body(0, True, False, True)
            with dve.Fori(1, NB - 2) as j:
                body(j, True, True, True)
            body(NB - 2, True, True, False)
            body(NB - 1, False, True, False)
            body(NB, False, True, False, end=True)

            slot_columns(COLS // 2, COLS)
            finish_slots()

            def e_middle(k):
                dve.wait_ge(e_tanh, k + 1)
                V.scalar_tensor_tensor(out=u_e, in0=tanh_e, scalar=1.0, in1=st_ps[:, :, 0:HF],
                                       op0=ALU.add, op1=ALU.mult).then_inc(e_u, 1)
                dve.wait_ge(e_u, k + 1)
                if not (isinstance(k, int) and k == 0):
                    dve.wait_ge(e_midT, k)
                dve.wait_ge(e_up, k + 1)
                V.scalar_tensor_tensor(out=mid_e, in0=u_e, scalar=0.5, in1=sm_ps[:, :, 0:HF],
                                       op0=ALU.mult, op1=ALU.mult).then_inc(e_mid, 1)

            def e_mid_transposed(k):
                dve.wait_ge(e_midT, k + 1)
                if not (isinstance(k, int) and k == 0):
                    dve.wait_ge(e_down, k)
                V.tensor_copy(midT_e[:, 4 * P:5 * P], work[:, 1, 0:P]).then_inc(e_midT_b, 1)
                V.tensor_copy(midT_e[0:FT[-1], 5 * P:6 * P], work[0:FT[-1], 1, P:2 * P]).then_inc(e_midT_b, 1)

            e_middle(0)
            with dve.Fori(1, TILES) as k:
                e_mid_transposed(k - 1)
                e_middle(k)
            e_mid_transposed(TILES - 1)

        @block.tensor
        def _(pe):
            MM = nc.tensor.matmul

            def three_passes(out_, pairs, start=True, stop=True):
                terms = [(a[i], b[k]) for a, b in pairs for i, k in ((0, 0), (0, 1), (1, 0))]
                for n, (a, b) in enumerate(terms):
                    last = MM(out_, a, b, start=(start and n == 0), stop=(stop and n == len(terms) - 1))
                return last

            def transposes(phase, j, kind, n, b, src, c):
                wait_bank(pe, phase, j, kind, n)
                for t in range(NT):
                    last = nc.tensor.transpose(bank(kind, n)[:, t * P:(t + 1) * P], src[:, t, c * P:(c + 1) * P],
                                               ident[:, :])
                last.then_inc(made[kind].sem, 1)

            def project_qk(phase, j, b, m):
                wait_bank(pe, phase, j, "qk", m)
                pe.wait_ge(taken["xT"].sem, taken["xT"].at(b))
                three_passes(bank("qk", m)[:, 0:TOK],
                             [([w[:, c, m * P:(m + 1) * P] for w in wqkv], [a[:, c, :] for a in xT]) for c in range(DC)]
                             ).then_inc(made["qk"].sem, 1)

            def project_v(phase, j, b, t):
                wait_bank(pe, phase, j, "v", t)
                three_passes(bank("v", t)[:, 0:D],
                             [([a[:, c, t * P:(t + 1) * P] for a in xT], [w[:, c, 2 * D:3 * D] for w in wqkv])
                              for c in range(DC)]).then_inc(made["v"].sem, 1)

            def search_scores(b, g, i):
                hh, t = divmod(i, NT)
                n = 12 * g + i
                if i == 0:
                    pe.wait_ge(stack_in[g].sem, stack_in[g].at(b))
                if not (isinstance(b, int) and b == 0 and n < 2):
                    pe.wait_ge(smax_found.sem, smax_found.at(b, n - 2))
                MM(sm_ps[:, n % 2, 0:TOK], q_st[0:KROWS, G * g + hh, t * P:(t + 1) * P], k_st[0:KROWS, G * g + hh, :],
                   start=True, stop=True).then_inc(smax_made.sem, 1)

            def transpose_shift(phase, j, b, g):
                wait_bank(pe, phase, j, "shift", g)
                pe.wait_ge(shift_split.sem, shift_split.at(b, g))
                dst = bank("shift", g).bitcast(BF16)
                for t in range(NT):
                    last = nc.tensor.transpose(dst[0:3 * G, t * P:(t + 1) * P],
                                               shift_p[:, t, :, :].rearrange("p a h -> p (a h)"), identb[:, :])
                last.then_inc(made["shift"].sem, 1)

            def scores(j, step, half):
                g, kc = divmod(step, NT)
                if kc == 0 and half == 0:
                    pe.wait_ge(shift_in[g].sem, shift_in[g].at(j))
                for hh in (2 * half, 2 * half + 1):
                    n = 4 * step + hh
                    if not (isinstance(j, int) and j == 0 and n < 2):
                        pe.wait_ge(exp_made.sem, exp_made.at(j, n - 2))
                    MM(st_ps[:, hh % 2, 0:TOK], k_st[0:KROWS + 3, G * g + hh, kc * P:(kc + 1) * P],
                       q_st[0:KROWS + 3, G * g + hh, :], start=True, stop=True).then_inc(st_made.sem, 1)

            def weigh_values(j, step):
                g, kc = divmod(step, NT)
                if step == 0:
                    pe.wait_ge(taken["v"].sem, taken["v"].at(j))
                if kc == 0 and not (isinstance(j, int) and j == 0 and g == 0):
                    pe.wait_ge(ot_copied.sem, ot_copied.at(j, g - 1))
                pe.wait_ge(exp_made.sem, exp_made.at(j, 4 * step + 3))
                for hh in range(G):
                    last = MM(pv_ps[2 * DH * hh:2 * DH * (hh + 1), 0:TOK], v_sb[:, kc, G * g + hh, :],
                              probs[:, step % 3, hh, :], start=(kc == 0), stop=(kc == NT - 1))
                last.then_inc(pv_made.sem, 1)

            def transpose_back(phase, j, b, g):
                wait_bank(pe, phase, j, "attn_back", g)
                pe.wait_ge(ot_copied.sem, ot_copied.at(b, g))
                for t in range(NT):
                    last = nc.tensor.transpose(bank("attn_back", g)[:, t * P:(t + 1) * P], ot[:, t * P:(t + 1) * P],
                                               ident[:, :])
                last.then_inc(made["attn_back"].sem, 1)

            def project_out(phase, j, b, t):
                wait_bank(pe, phase, j, "proj", t)
                pe.wait_ge(taken["attnT"].sem, taken["attnT"].at(b))
                three_passes(bank("proj", t)[:, 0:D],
                             [([a[:, c, t * P:(t + 1) * P] for a in attnT], [w[:, c, :] for w in wo])
                              for c in range(DC)]).then_inc(made["proj"].sem, 1)

            def router_scores(phase, j, b):
                wait_bank(pe, phase, j, "router", 0)
                pe.wait_ge(taken["x2T"].sem, taken["x2T"].at(b))
                three_passes(bank("router", 0)[0:E, 0:TOK],
                             [([w[:, c, :] for w in wr], [a[:, c, :] for a in x2T]) for c in range(DC)]
                             ).then_inc(router_made.sem, 1)

            def turn_scores(b):
                pe.wait_ge(router_copied.sem, router_copied.at(b))
                pe.sem_inc(pe_passed, 1)
                for t in range(NT):
                    last = nc.tensor.transpose(bank("router", 0)[:, TOK + t * E:TOK + (t + 1) * E],
                                               router_T[:, t * P:(t + 1) * P], ident[0:E, 0:E])
                last.then_inc(made["router"].sem, 1)

            def shared_up(phase, j, b, f, kind, w):
                wait_bank(pe, phase, j, kind, f)
                three_passes(bank(kind, f)[0:FT[f], 0:TOK],
                             [([a[:, c, f * P:f * P + FT[f]] for a in w], [a[:, c, :] for a in x2T])
                              for c in range(DC)]).then_inc(made[kind].sem, 1)

            def shared_down(phase, j, b, t):
                wait_bank(pe, phase, j, "down", t)
                pairs = [([a[0:FT[f], f, t * P:(t + 1) * P] for a in mid], [w[0:FT[f], f, :] for w in wd])
                         for f in range(NF)]
                pe.wait_ge(mid_low.sem, mid_low.at(b, NF - 2))
                three_passes(bank("down", t)[:, 0:D], pairs[:-1], stop=False)
                pe.wait_ge(mid_low.sem, mid_low.at(b))
                three_passes(bank("down", t)[:, 0:D], pairs[-1:], start=False).then_inc(made["down"].sem, 1)

            def rank_tokens():
                pe.wait_ge(onehot_made, 1)
                hot = onehot.rearrange("p c e -> p (c e)")
                MM(sm_ps[:, 0, 0:COLS * E], before[:, :], hot, start=True, stop=False)
                for c in range(1, COLS):
                    MM(sm_ps[:, 0, c * E:COLS * E], onesb[:, :], hot[:, 0:(COLS - c) * E], start=False,
                       stop=(c == COLS - 1))
                for c in range(COLS):
                    last = MM(sm_ps[:, 1, 0:E], onesb[:, :], hot[:, c * E:(c + 1) * E], start=(c == 0),
                              stop=(c == COLS - 1))
                last.then_inc(rank_made, 1)

            def slot_numbers(first, end):
                for c in range(first, end):
                    pe.wait_ge(slot_cols, 2 + c + 1)
                    MM(st_ps[:, 0, 0:2 * TILES], slot_hot[:, c % 12, :], tile_val[:, c].rearrange("p i t -> p (i t)"),
                       start=(c == 0), stop=(c == COLS - 1)).then_inc(slots_read, 1)

            pe.wait_ge(consts_made, FIRST_CONSTS)
            pe.wait_ge(lora_in, 16 * NB)
            pe.wait_ge(small_in, 32)
            for n in range(2):
                for i in range(4):
                    last = nc.tensor.transpose(bank("loraT", n)[0:RANK, i * P:(i + 1) * P], lora_a[:, 4 * n + i, :],
                                               ident[:, :])
                last.then_inc(made["loraT"].sem, 1)
            for n in range(4):
                if n == 0:
                    pe.wait_ge(taken["loraT"].sem, 2)
                wait_bank(pe, "prologue", -1, "lora", n)
                for i in range(2):
                    bt = 2 * n + i
                    last = MM(bank("lora", n)[:, i * D:(i + 1) * D], lora_aT[:, bt * P:(bt + 1) * P], lora_b,
                              start=True, stop=True)
                last.then_inc(made["lora"].sem, 1)
            pe.wait_ge(w_split, 1)
            pe.wait_ge(ln_done[0].sem, ln_done[0].at(0))
            for c in range(DC):
                transposes("prologue", -1, "xT", c, 0, xn, c)
            for m in (0, 2, 1, 3):
                project_qk("prologue", -1, 0, m)
            for i in range(12):
                search_scores(0, 0, i)
            transpose_shift("prologue", -1, 0, 0)
            for i in range(12):
                search_scores(0, 1, i)
            for t in range(NT):
                project_v("prologue", -1, 0, t)
            pe.wait_ge(w_split, SPLITS)
            pe.wait_ge(consts_made, CORE_CONSTS)

            def body(phase, j, front, back, end=False):
                f, b = j + 1, j - 1
                for q in range(HALVES + 1):
                    tail = q == HALVES
                    if not end and not tail:
                        scores(j, q // 2, q % 2)
                    if not end and q in (6, 12, 18):
                        weigh_values(j, q // 2 - 1)
                    if not end and tail:
                        weigh_values(j, 11)
                    if not end and not tail and (q < 12 or front):
                        bb, g = [(j, 2), (j, 3), (f, 0), (f, 1)][q // 6]
                        search_scores(bb, g, 2 * (q % 6))
                        search_scores(bb, g, 2 * (q % 6) + 1)
                    if q == 10 and back:
                        turn_scores(b)
                    for at_q, what, n, ahead in USES:
                        if at_q != q or not {1: front, 0: not end, -1: back}[ahead]:
                            continue
                        if what == "attn_back":
                            transpose_back(phase, j, j + ahead, n)
                        elif what == "shift":
                            transpose_shift(phase, j, j + ahead, n)
                        elif what == "xT":
                            pe.wait_ge(ln_done[0].sem, ln_done[0].at(f))
                            transposes(phase, j, "xT", n, f, xn, n)
                        elif what == "attnT":
                            pe.wait_ge(taken["attn_back"].sem, taken["attn_back"].at(b))
                            transposes(phase, j, "attnT", n, b, attn, n)
                        elif what == "x2T":
                            pe.wait_ge(ln_done[1].sem, ln_done[1].at(b))
                            transposes(phase, j, "x2T", n, b, xn2, n)
                        elif what == "qk":
                            project_qk(phase, j, f, n)
                        elif what == "v":
                            project_v(phase, j, f, n)
                        elif what == "proj":
                            project_out(phase, j, b, n)
                        elif what == "router":
                            router_scores(phase, j, b)
                        elif what == "gate":
                            shared_up(phase, j, b, n, "gate", wg)
                        elif what == "up":
                            shared_up(phase, j, b, n, "up", wu)
                        elif what == "down":
                            shared_down(phase, j, b, n)
                    if not end and q % 2 == 1 and q % 6 != 1:
                        weigh_values(j, q // 2 - 1)
                    if end and q == 12:
                        rank_tokens()
                    if end and q == 23:
                        slot_numbers(0, COLS // 2)

            body(0, 0, True, False)
            with pe.Fori(1, NB - 2) as j:
                body("loop", j, True, True)
            body(NB - 2, NB - 2, True, True)
            body(NB - 1, NB - 1, False, True)
            body("end", NB, False, True, end=True)

            slot_numbers(COLS // 2, COLS)
            pe.wait_ge(routed, 1)

            def e_transpose(k, i, arrived):
                pe.wait_ge(row_in[i], arrived)
                if not (isinstance(k, int) and k == 0):
                    pe.wait_ge(e_xT_copied, k)
                for c in range(DC):
                    last = nc.tensor.transpose(pv_ps[:, c * P:(c + 1) * P], xg[:, i, c * P:(c + 1) * P], ident[:, :])
                last.then_inc(e_xT, 1)

            def e_gate_products(k):
                expert = pe.value_load(route_i[0:1, bass.ds(k, 1)], min_val=0, max_val=E - 1)
                place = pe.value_load(route_i[0:1, bass.ds(k + TILES, 1)], min_val=0, max_val=2)
                pe.wait_ge(expert_ready, expert + 1)
                pe.wait_ge(e_xT_copied, k + 1)
                if not (isinstance(k, int) and k == 0):
                    pe.wait_ge(e_u, k)
                e_wide(wx[0], st_ps, place).then_inc(e_gate_made, 1)
                return place

            def e_up_products(k, place):
                if not (isinstance(k, int) and k == 0):
                    pe.wait_ge(e_mid, k)
                e_wide(wx[1], sm_ps, place).then_inc(e_up, 1)

            def e_wide(w, dst, place):
                for half in range(2):
                    for c in range(DC):
                        last = MM(dst[:, half, 0:HF], xT_e[:, c * P:(c + 1) * P],
                                  w[:, bass.ds(place, 1), c, half * HF:(half + 1) * HF].rearrange("p a w -> p (a w)"),
                                  start=(c == 0), stop=(c == DC - 1))
                return last

            def e_transpose_mid(k):
                pe.wait_ge(e_mid, k + 1)
                if not (isinstance(k, int) and k == 0):
                    pe.wait_ge(e_midT_a, k)
                    pe.wait_ge(e_midT_b, 2 * k)
                for f in range(NF):
                    last = nc.tensor.transpose(work[0:FT[f], f // 4, (f % 4) * P:(f % 4 + 1) * P],
                                               mid_row[:, f * P:f * P + FT[f]], ident[:, :])
                last.then_inc(e_midT, 1)

            def e_down_products(k):
                place = pe.value_load(route_i[0:1, bass.ds(k + TILES, 1)], min_val=0, max_val=2)
                pe.wait_ge(e_midT_a, k + 1)
                pe.wait_ge(e_midT_b, 2 * k + 2)
                if not (isinstance(k, int) and k == 0):
                    pe.wait_ge(e_y, k)
                for f in range(NF):
                    last = MM(work[:, 2, 0:D], midT_e[0:FT[f], f * P:(f + 1) * P],
                              wx[2][0:FT[f], bass.ds(place, 1), f, :].rearrange("p a w -> p (a w)"),
                              start=(f == 0), stop=(f == NF - 1))
                last.then_inc(e_down, 1)

            def e_turn(k, i, arrived):
                place = e_gate_products(k)
                e_transpose_mid(k - 1)
                e_up_products(k, place)
                if arrived is not None:
                    e_transpose(k + 1, i, arrived)
                e_down_products(k - 1)

            e_transpose(0, 0, 16)
            e_up_products(0, e_gate_products(0))
            e_transpose(1, 1, 16)
            with pe.Fori(1, TILES - 2, 2) as k:
                e_turn(k, 0, 8 * k + 24)
                e_turn(k + 1, 1, 8 * k + 24)
            e_turn(TILES - 2, 0, 16 * ((TILES - 1) // 2 + 1))
            e_turn(TILES - 1, 1, None)
            e_transpose_mid(TILES - 1)
            e_down_products(TILES - 1)


def kernel(**inputs):
    import numpy as _np
    import concourse.bacc as _bacc
    from concourse import mybir as _mybir
    from concourse.bass_utils import run_bass_kernel_spmd as _run

    t = {k: _np.asarray(v) for k, v in inputs.items()}
    laid = {
        "x": t["x"], "x_txt": t["x_txt"], "scharr": t["L0_tok_scharr"],
        "base_rows": t["L0_txt_base_weight"].T, "lora_A": t["L0_txt_lora_A"], "lora_B": t["L0_txt_lora_B"],
        "w_qkvT": t["L0_attn_w_qkv"].T, "w_outT": t["L0_attn_w_out"].T, "router": t["L0_ffn_router_DE"],
        "w1": t["L0_ffn_w1_eDF"], "w3": t["L0_ffn_w3_eDF"], "w2": t["L0_ffn_w2_eFD"],
        "ws1": t["L0_ffn_ws1_DF"], "ws3": t["L0_ffn_ws3_DF"], "ws2": t["L0_ffn_ws2_FD"],
    }
    nc = _bacc.Bacc("TRN2", target_bir_lowering=False, num_devices=1)
    arrays, args = {}, []
    for name, a in laid.items():
        a = _np.ascontiguousarray(a)
        arrays[f"in_{name}_dram"] = a
        args.append(nc.dram_tensor(f"in_{name}_dram", a.shape, _mybir.dt.from_np(a.dtype), kind="ExternalInput").ap())
    shape = (t["x"].shape[0], t["x"].shape[2] + t["x_txt"].shape[1], t["x"].shape[3])
    args.append(nc.dram_tensor("out_0_dram", shape, _mybir.dt.float32, kind="ExternalOutput").ap())
    embed_block_moe_kernel(nc, *args)
    r = _run(nc, [arrays], core_ids=[0])
    return r.results[0]["out_0_dram"]
```
